# Optimizing a Trainium2 kernel written in Bass

```python
import numpy as np
import jax
import jax.numpy as jnp

def _softmax(x, axis=-1):
    return jax.nn.softmax(x, axis=axis)

def _gelu(x):
    return jax.nn.gelu(x, approximate=True)

def _silu(x):
    return jax.nn.silu(x)

def _sigmoid(x):
    return jax.nn.sigmoid(x)

def _layernorm(x, axis=-1, eps=1e-05):
    m = jnp.mean(x, axis=axis, keepdims=True)
    v = jnp.var(x, axis=axis, keepdims=True)
    return (x - m) / jnp.sqrt(v + eps)

def _scatter_add(tgt, idx, src, axis=0):
    return tgt.at[idx].add(src)

def _segment_sum(src, seg, n):
    return jax.ops.segment_sum(src, seg, n)
kernel_name = 'mk_prb_d1_jaxref_r4_01e920'

def setup_inputs(seed: int=0):
    np.random.seed(seed)
    _w = jnp.asarray

    def _L0_attn_setup():
        import jax, jax.numpy as jnp
        import numpy as np
        B, N, C = (2, 512, 256)
        H = 16
        D = C // H
        key = jax.random.key(seed)
        ks = jax.random.split(key, 5)
        s = 0.02
        return {'x': jax.random.normal(ks[0], (B, N, C), dtype=jnp.float32), 'qkv_w': jax.random.normal(ks[1], (C, 3 * C), dtype=jnp.float32) * s, 'qkv_b': jax.random.normal(ks[2], (3 * C,), dtype=jnp.float32) * s, 'proj_w': jax.random.normal(ks[3], (C, C), dtype=jnp.float32) * s, 'proj_b': jax.random.normal(ks[4], (C,), dtype=jnp.float32) * s}
    _L0_attn_in = _L0_attn_setup()

    def _L0_ffn_setup():
        import jax, jax.numpy as jnp
        import numpy as np
        DIM = 256
        HIDDEN = 768
        SCALE = 1.0 / 127.0

        def _dequant(w_int, dtype):
            return w_int.astype(dtype) * jnp.asarray(SCALE, dtype)
        key = jax.random.key(seed)
        k_x, k_g, k_u, k_d = jax.random.split(key, 4)
        x = jax.random.normal(k_x, (4, 512, DIM), dtype=jnp.float32)
        w_gate = jax.random.randint(k_g, (HIDDEN, DIM), -127, 128, dtype=jnp.int32)
        w_up = jax.random.randint(k_u, (HIDDEN, DIM), -127, 128, dtype=jnp.int32)
        w_down = jax.random.randint(k_d, (DIM, HIDDEN), -127, 128, dtype=jnp.int32)
        return {'x': x, 'w_gate': w_gate, 'w_up': w_up, 'w_down': w_down}
    _L0_ffn_in = _L0_ffn_setup()
    _d = {'L0_attn_x': _L0_attn_in['x'], 'L0_attn_qkv_w': _L0_attn_in['qkv_w'], 'L0_attn_qkv_b': _L0_attn_in['qkv_b'], 'L0_attn_proj_w': _L0_attn_in['proj_w'], 'L0_attn_proj_b': _L0_attn_in['proj_b'], 'L0_ffn_w_gate': _L0_ffn_in['w_gate'], 'L0_ffn_w_up': _L0_ffn_in['w_up'], 'L0_ffn_w_down': _L0_ffn_in['w_down']}
    _x0 = _d['L0_attn_x']
    _d['L0_attn_x'] = jax.random.normal(jax.random.fold_in(jax.random.key(seed), 1), (8, 512, 256), dtype=_x0.dtype)
    del _x0
    return _d

def reference(L0_attn_x, L0_attn_qkv_w, L0_attn_qkv_b, L0_attn_proj_w, L0_attn_proj_b, L0_ffn_w_gate, L0_ffn_w_up, L0_ffn_w_down):

    def _L0_attn_ref(x, qkv_w, qkv_b, proj_w, proj_b):
        import jax, jax.numpy as jnp
        import numpy as np
        B, N, C = (2, 512, 256)
        H = 16
        D = C // H
        b, n, c = x.shape
        scale = (c // H) ** (-0.5)
        qkv = x @ qkv_w + qkv_b
        qkv = qkv.reshape(b, n, 3, H, D)
        q, k, v = jnp.moveaxis(qkv, 2, 0)
        attn = jnp.einsum('bnhd,bmhd->bhnm', q, k) * scale
        attn = jax.nn.softmax(attn, axis=-1)
        out = jnp.einsum('bhnm,bmhd->bnhd', attn, v).reshape(b, n, c)
        out = out @ proj_w + proj_b
        return out

    def _L0_ffn_ref(x, w_gate, w_up, w_down):
        import jax, jax.numpy as jnp
        import numpy as np
        DIM = 256
        HIDDEN = 768
        SCALE = 1.0 / 127.0

        def _dequant(w_int, dtype):
            return w_int.astype(dtype) * jnp.asarray(SCALE, dtype)
        wg = _dequant(w_gate, x.dtype)
        wu = _dequant(w_up, x.dtype)
        wd = _dequant(w_down, x.dtype)
        gate = jnp.einsum('bsd,hd->bsh', x, wg)
        up = jnp.einsum('bsd,hd->bsh', x, wu)
        h = jax.nn.silu(gate) * up
        return jnp.einsum('bsh,dh->bsd', h, wd)
    x = L0_attn_x
    xn = _layernorm(x, axis=-1)
    x = x + _L0_attn_ref(xn, L0_attn_qkv_w, L0_attn_qkv_b, L0_attn_proj_w, L0_attn_proj_b) + _L0_ffn_ref(xn, L0_ffn_w_gate, L0_ffn_w_up, L0_ffn_w_down)
    return x

_drawn_inputs = setup_inputs


def setup_inputs(seed=0):
    import zlib

    import numpy as np

    out = dict(_drawn_inputs(seed))
    spreads = {}
    factors = {'L0_attn_qkv_w': 64.0,
     'L0_attn_qkv_b': 64.0,
     'L0_attn_proj_w': 64.0,
     'L0_attn_proj_b': 64.0}
    for name, (base, spread) in spreads.items():
        noise = np.random.default_rng([zlib.crc32(name.encode()), seed]).standard_normal(out[name].shape)
        drawn = base * np.exp(spread * noise) if base else spread * noise
        out[name] = jnp.asarray(drawn.astype(out[name].dtype))
    for name, factor in factors.items():
        out[name] = (out[name] * factor).astype(out[name].dtype)
    return out
```

```python
from contextlib import ExitStack

import concourse.bass as bass
from concourse import mybir

F32 = mybir.dt.float32
F32R = mybir.dt.float32r
I32 = mybir.dt.int32
ALU = mybir.AluOpType
ACT = mybir.ActivationFunctionType
AX_X = mybir.AxisListType.X

P = 128
ROWS = 8
TOK = 512
NT = TOK // P
C = 256
KC = C // P
HEADS = 16
HD = C // HEADS
HG = 4
NG = HEADS // HG
HID = 768
KH = HID // P
STEPS = NG * NT
LEAD = 6
SCALE = float(HD) ** -0.5
QUANT = 1.0 / 127.0
EPS = 1e-5
ONES_ROW = 96
STACK = ONES_ROW + 2
DENSE_BANKS = 3
PV_SLOT = 1
O_SLOT = 2

CHUNKS = [
    (0, 1, "v", 0, 0), (0, 3, "v", 1, 0),
    (1, 1, "gate", 3, 0), (1, 2, "o", 3, -1), (1, 3, "up", 3, 0),
    (2, 1, "ot", 0, -1), (2, 2, "ot", 1, -1), (2, 3, "max", 1, 0),
    (3, 1, "proj", 0, -1), (3, 3, "proj", 1, -1),
    (4, 1, "gate", 4, 0), (4, 3, "up", 4, 0),
    (5, 0, "gate", 5, 0), (5, 1, "up", 5, 0), (5, 2, "o", 0, 0), (5, 3, "xn", 0, 1),
    (6, 0, "xn", 1, 1), (6, 2, "max", 2, 0), (6, 3, "q", 0, 1),
    (7, 1, "k", 0, 1), (7, 3, "down", 0, 0),
    (8, 1, "q", 1, 1), (8, 3, "k", 1, 1),
    (9, 1, "down", 1, 0), (9, 2, "o", 1, 0), (9, 3, "down", 2, 0),
] + [(9, 3, w, i, None) for w in ("wgate", "wup", "wdown") for i in range(3)] + [
    (10, 1, "down", 3, 0), (10, 2, "max", 3, 0),
    (11, 1, "gate", 0, 1), (11, 3, "up", 0, 1),
    (12, 1, "gate", 1, 1),
    (13, 1, "up", 1, 1), (13, 2, "o", 2, 0),
    (14, 1, "gate", 2, 1), (14, 2, "max", 0, 1),
    (15, 1, "up", 2, 1),
]
WPREP = ("wgate", "wup", "wdown")
ON_ACT = ("xn", "q", "k", "max", "ot", "gate") + WPREP
ALL = tuple({kind for _, _, kind, _, _ in CHUNKS})


class Row:

    def __init__(self, at, like):
        self.at, self.like = at, like

    def has(self, offset):
        return 0 <= self.like + offset < ROWS

    def exists(self, chunk):
        return self.like == -1 if chunk[4] is None else self.has(chunk[4])


def rows_of(engine, step):
    step(Row(-1, -1))
    step(Row(0, 0))
    with engine.Fori(1, ROWS - 1) as b:
        step(Row(b, 1))
    step(Row(ROWS - 1, ROWS - 1))
    step(Row(ROWS, ROWS))


def count(row, kinds, chunk=None, kind=None, index=None):
    like = row.like
    if chunk is None:
        (chunk,) = [c for c in CHUNKS if c[2] == kind and c[3] == index]
    last = CHUNKS.index(chunk)
    total = 0
    for r in range(-1, like + 1):
        for n, c in enumerate(CHUNKS):
            if c[2] in kinds and Row(r, r).exists(c) and (r < like or n <= last):
                total += 1
    per = sum(c[2] in kinds and c[4] is not None for c in CHUNKS)
    return total + per * (row.at - row.like)


def build(nc, x, qkv_w, qkv_b, proj_w, proj_b, w_gate, w_up, w_down, out):
    x_rows = x.rearrange("b (t p) c -> b p t c", p=P)
    out_rows = out.rearrange("b (t p) c -> b p t c", p=P)
    q_spread = nc.dram_tensor("q_spread", [HEADS, 2, HD, TOK], F32, kind="Internal").ap()
    k_spread = nc.dram_tensor("k_spread", [HEADS, 3, HD, TOK], F32, kind="Internal").ap()

    with ExitStack() as ctx:
        def sb(name, shape, dt=F32):
            return ctx.enter_context(nc.sbuf_tensor(name, shape, dt))

        def ps(name, shape):
            return ctx.enter_context(nc.psum_tensor(name, shape, F32))

        def sem(name):
            return ctx.enter_context(nc.semaphore(name))

        w_qkv = [sb(f"w_qkv{i}", [P, KC, 3 * C], F32R) for i in "hl"]
        w_g = [sb(f"w_g{i}", [P, KC, HID], F32R) for i in "hl"]
        w_u = [sb(f"w_u{i}", [P, KC, HID], F32R) for i in "hl"]
        w_d = [sb(f"w_d{i}", [P, KH, C], F32R) for i in "hl"]
        w_p = [sb(f"w_p{i}", [P, KC, C], F32R) for i in "hl"]
        qk_bias = sb("qk_bias", [P, 2 * KC])
        v_bias = sb("v_bias", [P, C])
        p_bias = sb("p_bias", [P, C])
        ident = sb("ident", [P, P])
        xn = sb("xn", [P, NT, C])
        stats = sb("stats", [P, NT, 6])
        moments = sb("moments", [P, NT, 2])
        rstd = sb("rstd", [P, NT])
        minus_half = sb("minus_half", [P, NT])
        eps = sb("eps", [P, NT])
        xn_t = [sb(f"xn_t{i}", [P, KC, TOK], F32R) for i in "hl"]
        qk_parts = sb("qk_parts", [P, 2, 2, TOK], F32R)
        q_stack = sb("q_stack", [P, NG, HG, TOK], F32R)
        k_stack = sb("k_stack", [P, NG, HG, TOK], F32R)
        v_ones = sb("v_ones", [P, NT, HEADS, 2 * HD])
        probs = sb("probs", [P, 2, HG, TOK])
        neg_max = sb("neg_max", [P, 2, HG * NT])
        max_t = [sb(f"max_t{i}", [HG * NT, P], F32R) for i in "hl"]
        o_raw = sb("o_raw", [P, TOK])
        inv_sum = sb("inv_sum", [P, NT, HG])
        o_norm = sb("o_norm", [P, NT, C])
        gated = sb("gated", [P, TOK])
        hid = sb("hid", [P, 2, TOK])
        hid_t = [sb(f"hid_t{i}", [P, KH, TOK], F32R) for i in "hl"]
        resid = sb("resid", [P, NT, C])
        raw = probs[:, :, :, :].rearrange("p a h n -> p (a h n)")
        raw_qkv = raw[:, 0:KC * 3 * C].rearrange("p (k n) -> p k n", k=KC)
        raw_p = raw[:, KC * 3 * C:KC * 4 * C].rearrange("p (k n) -> p k n", k=KC)
        raw_g = raw[:, KC * 4 * C:KC * 4 * C + KH * C]
        raw_u = v_ones[:, :, :, :].rearrange("p a h n -> p (a h n)")[:, 0:KH * C]
        raw_d = raw[:, 0:KH * C]

        st_bank = [ps(f"st_bank{i}", [P, TOK]) for i in range(2)]
        s_bank = [ps(f"s_bank{i}", [P, TOK]) for i in range(2)]
        o_bank = ps("o_bank", [P, TOK])
        dense = [ps(f"dense{i}", [P, TOK]) for i in range(DENSE_BANKS)]

        w_in = [sem(f"w_in_{n}") for n in ("qkv", "p", "g", "u", "d")]
        bias_in = sem("bias_in")
        x_in = sem("x_in")
        resid_in = sem("resid_in")
        spread = [sem(f"spread{i}") for i in range(2)]
        stack_in = [sem(f"stack_in{g}") for g in range(NG)]
        max_in = [sem(f"max_in{g}") for g in range(NG)]
        out_done = sem("out_done")
        ident_zero = sem("ident_zero")
        ident_ready = sem("ident_ready")
        const_pool = sem("const_pool")
        w_high = sem("w_high")
        w_low = sem("w_low")
        w_float = sem("w_float")
        st_done = sem("st_done")
        exp_done = sem("exp_done")
        s_done = sem("s_done")
        max_done = sem("max_done")
        pv_done = sem("pv_done")
        o_raw_done = sem("o_raw_done")
        inv_done = sem("inv_done")
        dense_done = sem("dense_done")
        act_done = sem("act_done")
        dense_free = sem("dense_free")
        hid_high = sem("hid_high")
        hid_low = sem("hid_low")
        stats_done = sem("stats_done")
        moments_done = sem("moments_done")
        var_done = sem("var_done")
        rstd_done = sem("rstd_done")
        xn_done = sem("xn_done")
        resid_ready = sem("resid_ready")

        block = ctx.enter_context(nc.Block())

        def bank_of(row, chunk):
            return dense[(count(Row(row.like, row.like), ALL, chunk) - 1) % DENSE_BANKS]

        def chunks_at(row, step, slot):
            return [c for c in CHUNKS if c[:2] == (step, slot) and row.exists(c)]

        def head_ahead(row, step):
            s = step + LEAD
            if not 0 <= STEPS * row.like + s < STEPS * ROWS:
                return None
            return s % STEPS // HG, s % HG, STEPS * row.at + s, s // STEPS

        def of_row(row, offset):
            return Row(row.at + offset, row.like + offset)

        def weight_place(kind, i):
            w = {"wgate": w_g, "wup": w_u, "wdown": w_d}[kind]
            if kind == "wdown":
                return w, (slice(None), slice(2 * i, 2 * i + 2), slice(None))
            return w, (slice(None), slice(None), slice(C * i, C * (i + 1)))

        @block.sync
        def _(sp):
            def load_x(at):
                sp.dma_start(xn[:, :, :], x_rows[at]).then_inc(x_in, 16)

            def raw_weight(n, dst, src):
                sp.dma_start(dst, src).then_inc(w_in[n], 16)

            def spread_heads(row, i):
                sp.wait_ge(dense_free, count(row, ALL, kind="k", index=i))
                heads = slice(2 * HG * i, 2 * HG * (i + 1))
                for part in range(2):
                    sp.dma_start(q_spread[heads, part], qk_parts[:, 0, part, :].bitcast(F32)).then_inc(spread[i], 16)
                for part, half in ((0, 0), (1, 1), (2, 0)):
                    sp.dma_start(k_spread[heads, part], qk_parts[:, 1, half, :].bitcast(F32))\
                      .then_inc(spread[i], 16)

            def heads_spread(row, i):
                sp.wait_ge(spread[i], 80 * (row.at + 2))

            def load_stack(row, g):
                if row.has(0) and g > 0:
                    sp.wait_ge(st_done, 64 * row.at + 16 * (g + 1))
                heads = slice(HG * g, HG * (g + 1))
                for half in range(2):
                    rows = slice(2 * HD * half, 2 * HD * (half + 1))
                    sp.dma_start(q_stack[rows, g].bitcast(F32), q_spread[heads].rearrange("h a d n -> (a d) h n"))\
                      .then_inc(stack_in[g], 16)
                    sp.dma_start(k_stack[rows, g].bitcast(F32),
                                 k_spread[heads, half:half + 2].rearrange("h a d n -> (a d) h n"))\
                      .then_inc(stack_in[g], 16)

            def load_max(row, g, meanwhile=None):
                sp.wait_ge(dense_free, count(row, ALL, kind="max", index=g))
                for part in range(2):
                    at = ONES_ROW + part
                    if meanwhile is not None and part == 1:
                        heads_spread(row, meanwhile)
                    sp.dma_start(q_stack[at:at + 1, g].bitcast(F32), max_t[part][:, :].bitcast(F32))\
                      .then_inc(max_in[g], 16)

            def step(row):
                if row.like == -1:
                    load_x(0)
                    raw_weight(0, raw_qkv, qkv_w.rearrange("(k p) n -> p k n", p=P))
                    sp.dma_start(qk_bias[:, :], qkv_b[0:2 * C].rearrange("(k p) -> p k", p=P),
                                 allow_slow_non_contiguous=True).then_inc(bias_in, 16)
                    sp.dma_start(v_bias[:, :], qkv_b[2 * C:3 * C].partition_broadcast(P)).then_inc(bias_in, 16)
                    sp.dma_start(p_bias[:, :], proj_b.partition_broadcast(P)).then_inc(bias_in, 16)
                    raw_weight(1, raw_p, proj_w.rearrange("(k p) n -> p k n", p=P))
                    raw_weight(2, raw_g.bitcast(I32).rearrange("p (k n) -> p k n", n=C),
                               w_gate.rearrange("(k p) n -> p k n", p=P))
                    raw_weight(3, raw_u.bitcast(I32).rearrange("p (k n) -> p k n", n=C),
                               w_up.rearrange("(k p) n -> p k n", p=P))
                    sp.wait_ge(w_high, 2)
                    sp.wait_ge(w_low, 2)
                    raw_weight(4, raw_d.bitcast(I32).rearrange("p (k n) -> p k n", n=HID),
                               w_down.rearrange("(k p) n -> p k n", p=P))
                if row.has(0):
                    if row.has(1):
                        sp.wait_ge(dense_done, count(of_row(row, -1), ALL, kind="xn", index=1))
                        load_x(row.at + 1)
                    load_max(row, 1)
                if row.has(-1):
                    sp.wait_ge(dense_free, count(row, ALL, kind="proj", index=1))
                    sp.dma_start(out_rows[row.at - 1], resid[:, :, :]).then_inc(out_done, 16)
                    sp.wait_ge(out_done, 16 * row.at)
                if row.has(0):
                    sp.dma_start(resid[:, :, :], x_rows[row.at]).then_inc(resid_in, 16)
                    load_max(row, 2)
                if row.has(1):
                    spread_heads(row, 0)
                    heads_spread(row, 0)
                    load_stack(row, 0)
                    load_stack(row, 1)
                    spread_heads(row, 1)
                if row.has(0):
                    load_max(row, 3, meanwhile=1 if row.has(1) else None)
                elif row.has(1):
                    heads_spread(row, 1)
                if row.has(1):
                    load_stack(row, 2)
                    load_max(row, 0)
                    load_stack(row, 3)

            rows_of(sp, step)

        @block.gpsimd
        def _(pool):
            nc.gpsimd.memset(ident[:, :], 0.0).then_inc(ident_zero, 1)
            pool.wait_ge(ident_zero, 1)
            nc.gpsimd.affine_select(out=ident[:, :], in_=ident[:, :], compare_op=ALU.not_equal, fill=1.0, base=0,
                                    pattern=[[-1, P]], channel_multiplier=1).then_inc(ident_ready, 1)
            nc.gpsimd.memset(minus_half[:, :], -0.5)
            nc.gpsimd.memset(eps[:, :], EPS).then_inc(const_pool, 1)
            pool.wait_ge(const_pool, 1)

            def deviation(row):
                n = row.at + 1
                pool.wait_ge(moments_done, NT * (n + 1))
                nc.gpsimd.tensor_tensor(rstd[:, :], moments[:, :, 1], eps[:, :], ALU.add).then_inc(var_done, 1)
                pool.wait_ge(var_done, n + 1)
                nc.gpsimd.tensor_tensor(rstd[:, :], rstd[:, :], minus_half[:, :], ALU.pow).then_inc(rstd_done, 1)

            def hidden_low(row, chunk):
                n = count(row, ("up",), chunk)
                pool.wait_ge(dense_free, count(row, ALL, chunk))
                pool.wait_ge(hid_high, n)
                m = chunk[3]
                nc.gpsimd.tensor_tensor(hid_t[1][:, m, :], hid[:, m % 2, :], hid_t[0][:, m, :].bitcast(F32),
                                        ALU.subtract).then_inc(hid_low, 1)

            def step(row):
                if row.like == -1:
                    deviation(row)
                    pool.wait_ge(rstd_done, 1)
                    for g in range(NG):
                        nc.gpsimd.memset(k_stack[64:P, g].bitcast(F32), 1.0).then_inc(const_pool, 1)
                        pool.wait_ge(const_pool, 2 * g + 2)
                        nc.gpsimd.memset(q_stack[64:ONES_ROW, g].bitcast(F32), 0.0).then_inc(const_pool, 1)
                        pool.wait_ge(const_pool, 2 * g + 3)
                for s in range(STEPS):
                    if s == 1 and row.has(1) and row.like >= 0:
                        deviation(row)
                    if s == 10 and row.like == -1:
                        pool.wait_ge(dense_done, count(row, ALL, kind="wup", index=2))
                        nc.gpsimd.memset(v_ones[:, :, :, :], 1.0).then_inc(const_pool, 1)
                    if s == 5 and row.has(0):
                        pool.wait_ge(resid_in, 16 * (row.at + 1))
                        pool.wait_ge(bias_in, 48)
                        for t in range(NT):
                            nc.gpsimd.tensor_tensor(resid[:, t, :], resid[:, t, :], p_bias[:, :],
                                                    ALU.add).then_inc(resid_ready, 1)
                    for slot in range(4):
                        for chunk in chunks_at(row, s, slot):
                            if chunk[2] == "up":
                                hidden_low(row, chunk)

            rows_of(pool, step)

        @block.scalar
        def _(act):
            def split_high(n, dst, src):
                act.wait_ge(w_in[n], 16)
                nc.scalar.activation(dst, src, ACT.Copy).then_inc(w_high, 1)

            def exp(row, s, j):
                tile = 64 * row.at + 4 * s + j
                act.wait_ge(st_done, tile + 1)
                if j == 0 and 16 * row.like + s >= 2:
                    act.wait_ge(pv_done, 16 * row.at + s - 1)
                if row.like == 0 and s < 2:
                    act.wait_ge(dense_done, count(Row(-1, -1), ALL, kind="wdown", index=2))
                nc.scalar.activation(probs[:, s % 2, j, :], st_bank[j % 2][:, :], ACT.Exp,
                                     scale=SCALE).then_inc(exp_done, 1)

            def take(row, chunk):
                _, _, kind, i, _ = chunk
                bank = bank_of(row, chunk)
                act.wait_ge(dense_done, count(row, ALL, chunk))
                if kind == "xn":
                    nc.scalar.activation(xn_t[0][:, i, :], bank[:, :], ACT.Copy).then_inc(act_done, 1)
                elif kind in ("q", "k"):
                    which = 0 if kind == "q" else 1
                    if row.has(0) or i == 1:
                        act.wait_ge(spread[1 - i], 80 * (row.at + 1 + i))
                    act.wait_ge(bias_in, 48)
                    nc.scalar.activation(qk_parts[:, which, 0, :], bank[:, :], ACT.Identity,
                                         bias=qk_bias[:, KC * which + i:KC * which + i + 1]).then_inc(act_done, 1)
                elif kind == "max":
                    g = 4 * (row.at + chunk[4]) + i
                    if 4 * (row.like + chunk[4]) + i >= 1:
                        act.wait_ge(max_in[(i - 1) % NG], 32 * (row.at + (1 if i else 0) + chunk[4]))
                    nc.scalar.activation(max_t[0][:, :], bank[0:HG * NT, 0:P], ACT.Copy).then_inc(act_done, 1)
                elif kind == "ot":
                    if i == 0:
                        act.wait_ge(spread[1], 80 * (row.at + (1 if row.has(0) else 0)))
                    nc.scalar.activation(qk_parts[:, i, 0, :], bank[:, :], ACT.Copy).then_inc(act_done, 1)
                elif kind == "gate":
                    if not (row.like == -1 and i == 0):
                        act.wait_ge(dense_free, count(row, ALL, chunk) - 1)
                    nc.scalar.activation(gated[:, :], bank[:, :], ACT.Tanh, scale=0.5 * QUANT).then_inc(act_done, 1)
                else:
                    w, cols = weight_place(kind, i)
                    nc.scalar.activation(w[0][cols], bank[:, :].rearrange("p (a n) -> p a n", a=2),
                                         ACT.Copy).then_inc(act_done, 1)

            def hidden_high(row, chunk):
                act.wait_ge(dense_free, count(row, ALL, chunk))
                m = chunk[3]
                nc.scalar.activation(hid_t[0][:, m, :], hid[:, m % 2, :], ACT.Copy).then_inc(hid_high, 1)

            def step(row):
                if row.like == -1:
                    split_high(0, w_qkv[0][:, :, 0:C], raw_qkv[:, :, 0:C])
                    split_high(0, w_qkv[0][:, :, C:3 * C], raw_qkv[:, :, C:3 * C])
                    split_high(1, w_p[0][:, :, :], raw_p)
                for s in range(STEPS):
                    for slot in range(4):
                        if row.has(0):
                            exp(row, s, slot)
                        if slot == 0:
                            r = row if s else of_row(row, -1)
                            for chunk in CHUNKS:
                                if chunk[2] == "up" and chunk[0] == (s - 1) % STEPS and r.like >= -1 and r.exists(chunk):
                                    hidden_high(r, chunk)
                        for chunk in chunks_at(row, s, slot):
                            if chunk[2] in ON_ACT:
                                take(row, chunk)
                        if slot == O_SLOT and s % NT == 0 and 0 < 16 * row.like + s <= 16 * ROWS:
                            act.wait_ge(pv_done, 16 * row.at + s)
                            if 16 * row.like + s > 4:
                                g = (s // NT - 2) % NG
                                shift = -1 if s == 0 else 0
                                act.wait_ge(dense_done, count(of_row(row, shift), ALL, kind="o", index=g))
                            nc.scalar.activation(o_raw[:, :], o_bank[:, :], ACT.Copy).then_inc(o_raw_done, 1)

            rows_of(act, step)

        @block.vector
        def _(dve):
            def statistics(row):
                n = row.at + 1
                dve.wait_ge(x_in, 16 * (n + 1))
                for t in range(NT):
                    nc.vector.bn_stats(stats[:, t, :], xn[:, t, :]).then_inc(stats_done, 1)
                dve.wait_ge(stats_done, NT * (n + 1))

            def average():
                for t in range(NT):
                    nc.vector.bn_aggr(moments[:, t, :], stats[:, t, :]).then_inc(moments_done, 1)

            def normalise(row):
                dve.wait_ge(rstd_done, row.at + 2)
                for t in range(NT):
                    nc.vector.tensor_scalar(xn[:, t, :], xn[:, t, :], moments[:, t, 0:1], rstd[:, t:t + 1],
                                            ALU.subtract, ALU.mult).then_inc(xn_done, 1)

            def maximum(row, s, q):
                g, h, item, ahead = head_ahead(row, s)
                dve.wait_ge(s_done, 4 * item + q + 1)
                nc.vector.tensor_reduce(neg_max[:, g % 2, NT * h + q:NT * h + q + 1], s_bank[q % 2][:, :], AX_X,
                                        ALU.max, negate=True).then_inc(max_done, 1)

            def take(row, chunk):
                _, _, kind, i, offset = chunk
                bank = bank_of(row, chunk)
                if kind in ON_ACT:
                    dve.wait_ge(act_done, count(row, ON_ACT, chunk))
                else:
                    dve.wait_ge(dense_done, count(row, ALL, chunk))
                if kind == "xn":
                    nc.vector.tensor_tensor(xn_t[1][:, i, :], bank[:, :], xn_t[0][:, i, :].bitcast(F32),
                                            ALU.subtract).then_inc(dense_free, 1)
                elif kind in ("q", "k"):
                    which = 0 if kind == "q" else 1
                    nc.vector.scalar_tensor_tensor(qk_parts[:, which, 1, :], bank[:, :],
                                                   qk_bias[:, KC * which + i:KC * which + i + 1],
                                                   qk_parts[:, which, 0, :].bitcast(F32),
                                                   ALU.add, ALU.subtract).then_inc(dense_free, 1)
                elif kind == "v":
                    if i == 0 and row.has(-1):
                        dve.wait_ge(pv_done, 16 * row.at)
                    if i == 0 and row.like == 0:
                        dve.wait_ge(const_pool, 2 * NG + 2)
                        dve.wait_ge(bias_in, 48)
                    for u in range(2):
                        done = nc.vector.tensor_tensor(v_ones[:, 2 * i + u, :, 0:HD],
                                                       bank[:, C * u:C * (u + 1)].rearrange("p (h d) -> p h d", d=HD),
                                                       v_bias[:, :].rearrange("p (h d) -> p h d", d=HD), ALU.add)
                    done.then_inc(dense_free, 1)
                elif kind == "max":
                    nc.vector.tensor_tensor(max_t[1][:, :], bank[0:HG * NT, 0:P], max_t[0][:, :].bitcast(F32),
                                            ALU.subtract).then_inc(dense_free, 1)
                elif kind == "o":
                    heads = bank[:, :].rearrange("p (t h d) -> p t h d", t=NT, h=HG)
                    if 4 * (row.like + offset) + i >= 1:
                        dve.wait_ge(dense_free, count(row, ALL, chunk) - 1)
                    nc.vector.reciprocal(inv_sum[:, :, :], heads[:, :, :, HD]).then_inc(inv_done, 1)
                    dve.wait_ge(inv_done, 4 * (row.at + offset) + i + 1)
                    nc.vector.tensor_tensor(
                        o_norm[:, :, HG * HD * i:HG * HD * (i + 1)].rearrange("p t (h d) -> p t h d", d=HD),
                        heads[:, :, :, 0:HD], inv_sum[:, :, :].unsqueeze(3).broadcast_to([P, NT, HG, HD]),
                        ALU.mult).then_inc(dense_free, 1)
                elif kind == "ot":
                    nc.vector.tensor_tensor(qk_parts[:, i, 1, :], bank[:, :], qk_parts[:, i, 0, :].bitcast(F32),
                                            ALU.subtract).then_inc(dense_free, 1)
                elif kind == "gate":
                    nc.vector.scalar_tensor_tensor(gated[:, :], gated[:, :], 1.0, bank[:, :], ALU.add,
                                                   ALU.mult).then_inc(dense_free, 1)
                elif kind == "up":
                    n = count(row, ("up",), chunk)
                    if not (row.like == -1 and i < 2):
                        dve.wait_ge(hid_high, n - 2)
                        dve.wait_ge(hid_low, n - 2)
                    dve.wait_ge(dense_free, count(row, ALL, chunk) - 1)
                    nc.vector.scalar_tensor_tensor(hid[:, i % 2, :], bank[:, :], 0.5 * QUANT ** 3, gated[:, :],
                                                   ALU.mult, ALU.mult).then_inc(dense_free, 1)
                elif kind == "down":
                    if i == 0:
                        dve.wait_ge(resid_ready, NT * (row.at + 1))
                    nc.vector.tensor_tensor(resid[:, i, :], bank[:, 0:C], resid[:, i, :],
                                            ALU.add).then_inc(dense_free, 1)
                elif kind == "proj":
                    if i == 0:
                        dve.wait_ge(dense_free, count(of_row(row, -1), ALL, kind="down", index=3))
                    both = resid[:, 2 * i:2 * i + 2, :]
                    nc.vector.tensor_tensor(both, bank[:, :].rearrange("p (t n) -> p t n", t=2), both,
                                            ALU.add).then_inc(dense_free, 1)
                else:
                    w, cols = weight_place(kind, i)
                    nc.vector.tensor_tensor(w[1][cols],
                                            bank[:, :].rearrange("p (a n) -> p a n", a=2),
                                            w[0][cols].bitcast(F32), ALU.subtract).then_inc(dense_free, 1)

            def split_low(n, dst, src, high):
                dve.wait_ge(w_high, n)
                nc.vector.tensor_tensor(dst, src, high.bitcast(F32), ALU.subtract).then_inc(w_low, 1)

            def to_float(n, ints):
                dve.wait_ge(w_in[n], 16)
                nc.vector.tensor_copy(ints, ints.bitcast(I32)).then_inc(w_float, 1)

            def step(row):
                if row.like == -1:
                    statistics(row)
                    average()
                    normalise(row)
                    split_low(1, w_qkv[1][:, :, 0:C], raw_qkv[:, :, 0:C], w_qkv[0][:, :, 0:C])
                    split_low(2, w_qkv[1][:, :, C:3 * C], raw_qkv[:, :, C:3 * C], w_qkv[0][:, :, C:3 * C])
                for s in range(STEPS):
                    if s == 1 and row.like >= 0 and row.has(1):
                        statistics(row)
                    if s == 2 and row.like >= 0 and row.has(1):
                        normalise(row)
                    if row.like == -1 and s == 6:
                        to_float(2, raw_g)
                        to_float(3, raw_u)
                    if row.like == -1 and s == 8:
                        to_float(4, raw_d)
                        split_low(3, w_p[1][:, :, :], raw_p, w_p[0][:, :, :])
                    for slot in range(4):
                        if head_ahead(row, s):
                            maximum(row, s, slot)
                        if (s, slot) == (1, 0) and row.like >= 0 and row.has(1):
                            average()
                        for chunk in chunks_at(row, s, slot):
                            take(row, chunk)

            rows_of(dve, step)

        @block.tensor
        def _(pe):
            SPLIT = ((0, 0), (1, 0), (0, 1))

            def scores_t(row, s, j):
                g, kt = s // NT, s % NT
                tile = 64 * row.at + 4 * s + j
                if kt == 0 and j == 0:
                    pe.wait_ge(max_in[g], 32 * (row.at + 1))
                if 16 * row.like + s > 0 or j >= 2:
                    pe.wait_ge(exp_done, tile - 1)
                nc.tensor.matmul(st_bank[j % 2][:, :], k_stack[0:STACK, g, j, P * kt:P * (kt + 1)],
                                 q_stack[0:STACK, g, j, :], start=True, stop=True).then_inc(st_done, 1)

            def scores(row, s, q):
                g, h, item, ahead = head_ahead(row, s)
                if h == 0 and q == 0:
                    pe.wait_ge(stack_in[g], 64 * (row.at + ahead + 1))
                    if row.like + ahead == 0:
                        pe.wait_ge(const_pool, 2 * g + 3)
                if 16 * row.like + s + LEAD > 0 or q >= 2:
                    pe.wait_ge(max_done, 4 * item + q - 1)
                nc.tensor.matmul(s_bank[q % 2][:, :], q_stack[0:ONES_ROW, g, h, P * q:P * (q + 1)],
                                 k_stack[0:ONES_ROW, g, h, :], start=True, stop=True).then_inc(s_done, 1)

            def probs_v(row, s):
                g, kt = (s - 1) % STEPS // NT, (s - 1) % NT
                n = 16 * row.at + s
                pe.wait_ge(exp_done, 4 * n)
                if s == 1:
                    pe.wait_ge(dense_free, count(row, ALL, kind="v", index=1))
                if kt == 0 and 16 * row.like + s > 1:
                    pe.wait_ge(o_raw_done, 4 * row.at + s // NT)
                for j in range(HG):
                    done = nc.tensor.matmul(o_bank[32 * j:32 * (j + 1), :], v_ones[:, kt, HG * g + j, :],
                                            probs[:, (s - 1) % 2, j, :], start=kt == 0, stop=kt == NT - 1,
                                            tile_position=(0, 32 * j))
                done.then_inc(pv_done, 1)

            def product(bank, stationary, moving, tiles):
                for n, (a, b) in enumerate(SPLIT):
                    for k in range(tiles):
                        done = nc.tensor.matmul(bank, stationary(a, k), moving(b, k), start=n == 0 and k == 0,
                                                stop=n == len(SPLIT) - 1 and k == tiles - 1)
                return done

            def chunk_products(row, chunk):
                _, _, kind, i, offset = chunk
                bank = bank_of(row, chunk)
                n = count(row, ALL, chunk)
                if count(Row(row.like, row.like), ALL, chunk) > DENSE_BANKS:
                    pe.wait_ge(dense_free, n - DENSE_BANKS)
                if kind == "xn":
                    if i == 0:
                        pe.wait_ge(xn_done, NT * (row.at + 2))
                    for t in range(NT):
                        done = nc.tensor.transpose(bank[:, P * t:P * (t + 1)], xn[:, t, P * i:P * (i + 1)], ident[:, :])
                elif kind in ("q", "k"):
                    if kind == "q" and i == 0:
                        pe.wait_ge(dense_free, count(row, ALL, kind="xn", index=1))
                        if row.like == -1:
                            pe.wait_ge(w_low, 2)
                    base = (0 if kind == "q" else C) + P * i
                    done = product(bank[:, :], lambda a, k: w_qkv[a][:, k, base:base + P],
                                   lambda b, k: xn_t[b][:, k, :], KC)
                elif kind == "v":
                    for u in range(2):
                        t = 2 * i + u
                        done = product(bank[:, C * u:C * (u + 1)], lambda a, k: xn_t[a][:, k, P * t:P * (t + 1)],
                                       lambda b, k: w_qkv[b][:, k, 2 * C:3 * C], KC)
                elif kind == "max":
                    pe.wait_ge(max_done, 16 * (4 * (row.at + offset) + i + 1))
                    done = nc.tensor.transpose(bank[0:HG * NT, 0:P], neg_max[:, i % 2, :], ident[:, :])
                elif kind == "o":
                    pe.wait_ge(o_raw_done, 4 * (row.at + offset) + i + 1)
                    for t in range(NT):
                        done = nc.tensor.transpose(bank[:, P * t:P * (t + 1)], o_raw[:, P * t:P * (t + 1)], ident[:, :])
                elif kind == "ot":
                    if i == 0:
                        pe.wait_ge(dense_free, count(row, ALL, kind="o", index=3))
                    for t in range(NT):
                        done = nc.tensor.transpose(bank[:, P * t:P * (t + 1)], o_norm[:, t, P * i:P * (i + 1)], ident[:, :])
                elif kind in ("gate", "up"):
                    w = w_g if kind == "gate" else w_u
                    if row.like == -1 and i == 0:
                        pe.wait_ge(dense_free, count(row, ALL, kind="wdown", index=2))
                    done = product(bank[:, :], lambda a, k: w[a][:, k, P * i:P * (i + 1)],
                                   lambda b, k: xn_t[b][:, k, :], KC)
                elif kind == "down":
                    if i == 0:
                        pe.wait_ge(hid_high, KH * (row.at + 1))
                        pe.wait_ge(hid_low, KH * (row.at + 1))
                    done = product(bank[:, 0:C], lambda a, k: hid_t[a][:, k, P * i:P * (i + 1)],
                                   lambda b, k: w_d[b][:, k, :], KH)
                elif kind == "proj":
                    if i == 0:
                        pe.wait_ge(dense_free, count(row, ALL, kind="ot", index=1))
                    for u in range(2):
                        t = 2 * i + u
                        done = product(bank[:, C * u:C * (u + 1)], lambda a, k: qk_parts[:, k, a, P * t:P * (t + 1)],
                                       lambda b, k: w_p[b][:, k, :], KC)
                elif kind == "wdown":
                    pe.wait_ge(w_float, 3)
                    d = raw_d.rearrange("p (k n) -> p k n", n=HID)
                    for t in range(4):
                        m, c = 2 * i + t // 2, t % 2
                        done = nc.tensor.transpose(bank[:, P * t:P * (t + 1)], d[:, c, P * m:P * (m + 1)], ident[:, :])
                else:
                    pe.wait_ge(w_float, 1 if kind == "wgate" else 2)
                    w = (raw_g if kind == "wgate" else raw_u).rearrange("p (k n) -> p k n", n=C)
                    for t in range(4):
                        c, m = t // 2, 2 * i + t % 2
                        done = nc.tensor.transpose(bank[:, P * t:P * (t + 1)], w[:, m, P * c:P * (c + 1)], ident[:, :])
                done.then_inc(dense_done, 1)

            def step(row):
                if row.like == -1:
                    pe.wait_ge(ident_ready, 1)
                for s in range(STEPS):
                    for slot in range(4):
                        if row.has(0):
                            scores_t(row, s, slot)
                        for chunk in chunks_at(row, s, slot):
                            chunk_products(row, chunk)
                        if head_ahead(row, s):
                            scores(row, s, slot)
                        if slot == PV_SLOT and 0 < 16 * row.like + s <= 16 * ROWS:
                            probs_v(row, s)

            rows_of(pe, step)


_INS = ["L0_attn_x", "L0_attn_qkv_w", "L0_attn_qkv_b", "L0_attn_proj_w", "L0_attn_proj_b",
        "L0_ffn_w_gate", "L0_ffn_w_up", "L0_ffn_w_down"]


def kernel(**inputs):
    import numpy as _np
    import concourse.bacc as _bacc
    from concourse import mybir as _mybir
    from concourse.bass_utils import run_bass_kernel_spmd as _run

    nc = _bacc.Bacc("TRN2", target_bir_lowering=False, num_devices=1)
    arrays, args = {}, []
    for name in _INS:
        a = _np.ascontiguousarray(inputs[name])
        arrays[f"in_{name}"] = a
        args.append(nc.dram_tensor(f"in_{name}", a.shape, _mybir.dt.from_np(a.dtype), kind="ExternalInput").ap())
    out = nc.dram_tensor("out_0", (ROWS, TOK, C), F32, kind="ExternalOutput").ap()
    build(nc, *args, out)
    r = _run(nc, [arrays], core_ids=[0])
    return r.results[0]["out_0"]
```

```python
from contextlib import ExitStack

import concourse.bass as bass
from concourse import mybir

F32 = mybir.dt.float32
F32R = mybir.dt.float32r
I32 = mybir.dt.int32
ALU = mybir.AluOpType
ACT = mybir.ActivationFunctionType
AX_X = mybir.AxisListType.X

P = 128
ROWS = 8
TOK = 512
NT = TOK // P
C = 256
KC = C // P
HEADS = 16
HD = C // HEADS
HG = 4
NG = HEADS // HG
HID = 768
KH = HID // P
STEPS = NG * NT
LEAD = 6
SCALE = float(HD) ** -0.5
QUANT = 1.0 / 127.0
EPS = 1e-5
ONES_ROW = 96
STACK = ONES_ROW + 2
DENSE_BANKS = 3
PV_SLOT = 2
O_SLOT = 3
STATS_AT = 4
AVERAGE_AT = 8
NORMALISE_AT = 12
HIGH_DELAY = 2

CHUNKS = [
    (0, 1, 'v', 0, 0),
    (0, 3, 'v', 1, 0),
    (1, 1, 'o', 3, -1),
    (1, 2, 'gate', 3, 0),
    (1, 3, 'up', 3, 0),
    (2, 1, 'ot', 0, -1),
    (2, 2, 'ot', 1, -1),
    (2, 3, 'max', 1, 0),
    (3, 1, 'proj', 0, -1),
    (3, 3, 'proj', 1, -1),
    (4, 1, 'gate', 4, 0),
    (4, 3, 'up', 4, 0),
    (5, 0, 'gate', 5, 0),
    (5, 1, 'up', 5, 0),
    (5, 3, 'xn', 0, 1),
    (6, 0, 'xn', 1, 1),
    (6, 1, 'o', 0, 0),
    (6, 2, 'max', 2, 0),
    (6, 3, 'q', 0, 1),
    (7, 1, 'k', 0, 1),
    (7, 1, 'wgate', 0, None),
    (7, 1, 'wgate', 1, None),
    (7, 1, 'wgate', 2, None),
    (7, 1, 'wup', 0, None),
    (7, 1, 'wup', 1, None),
    (7, 1, 'wup', 2, None),
    (7, 1, 'wdown', 0, None),
    (7, 1, 'wdown', 1, None),
    (7, 1, 'wdown', 2, None),
    (7, 3, 'down', 0, 0),
    (8, 1, 'q', 1, 1),
    (8, 1, 'k', 1, 1),
    (8, 3, 'down', 1, 0),
    (9, 0, 'down', 2, 0),
    (9, 3, 'o', 1, 0),
    (10, 1, 'down', 3, 0),
    (10, 2, 'max', 3, 0),
    (11, 0, 'gate', 0, 1),
    (11, 3, 'up', 0, 1),
    (12, 1, 'gate', 1, 1),
    (13, 1, 'up', 1, 1),
    (13, 3, 'o', 2, 0),
    (14, 1, 'max', 0, 1),
    (14, 3, 'gate', 2, 1),
    (15, 1, 'up', 2, 1),
]
WPREP = ("wgate", "wup", "wdown")
ON_ACT = ("xn", "q", "k", "max", "ot", "gate") + WPREP
FIRST_MAXIMA = next(c for c in CHUNKS if c[2:] == ("max", 0, 1))
SQUARES_AFTER = ("up", 1)
DECISION_AFTER = ("max", 0)
ALL = tuple({kind for _, _, kind, _, _ in CHUNKS})


class Row:

    def __init__(self, at, like):
        self.at, self.like = at, like

    def has(self, offset):
        return 0 <= self.like + offset < ROWS

    def exists(self, chunk):
        return self.like == -1 if chunk[4] is None else self.has(chunk[4])


def rows_of(engine, step):
    step(Row(-1, -1))
    step(Row(0, 0))
    with engine.Fori(1, ROWS - 1) as b:
        step(Row(b, 1))
    step(Row(ROWS - 1, ROWS - 1))
    step(Row(ROWS, ROWS))


def count(row, kinds, chunk=None, kind=None, index=None):
    like = row.like
    if chunk is None:
        (chunk,) = [c for c in CHUNKS if c[2] == kind and c[3] == index]
    last = CHUNKS.index(chunk)
    total = 0
    for r in range(-1, like + 1):
        for n, c in enumerate(CHUNKS):
            if c[2] in kinds and Row(r, r).exists(c) and (r < like or n <= last):
                total += 1
    per = sum(c[2] in kinds and c[4] is not None for c in CHUNKS)
    return total + per * (row.at - row.like)


def build(nc, x, qkv_w, qkv_b, proj_w, proj_b, w_gate, w_up, w_down, out):
    x_rows = x.rearrange("b (t p) c -> b p t c", p=P)
    out_rows = out.rearrange("b (t p) c -> b p t c", p=P)
    q_spread = nc.dram_tensor("q_spread", [HEADS, 2, HD, TOK], F32, kind="Internal").ap()
    k_spread = nc.dram_tensor("k_spread", [HEADS, 3, HD, TOK], F32, kind="Internal").ap()

    with ExitStack() as ctx:
        def sb(name, shape, dt=F32):
            return ctx.enter_context(nc.sbuf_tensor(name, shape, dt))

        def ps(name, shape):
            return ctx.enter_context(nc.psum_tensor(name, shape, F32))

        def sem(name):
            return ctx.enter_context(nc.semaphore(name))

        w_qkv = [sb(f"w_qkv{i}", [P, KC, 3 * C], F32R) for i in "hl"]
        w_g = [sb(f"w_g{i}", [P, KC, HID], F32R) for i in "hl"]
        w_u = [sb(f"w_u{i}", [P, KC, HID], F32R) for i in "hl"]
        w_d = [sb(f"w_d{i}", [P, KH, C], F32R) for i in "hl"]
        w_p = [sb(f"w_p{i}", [P, KC, C], F32R) for i in "hl"]
        qk_bias = sb("qk_bias", [P, 2 * KC])
        v_bias = sb("v_bias", [P, C])
        p_bias = sb("p_bias", [P, C])
        ident = sb("ident", [P, P])
        xn = sb("xn", [P, NT, C])
        stats = sb("stats", [P, NT, 6])
        moments = sb("moments", [P, NT, 2])
        rstd = sb("rstd", [P, NT])
        minus_half = sb("minus_half", [P, NT])
        eps = sb("eps", [P, NT])
        xn_t = [sb(f"xn_t{i}", [P, KC, TOK], F32R) for i in "hl"]
        qk_parts = sb("qk_parts", [P, 2, 2, TOK], F32R)
        q_stack = sb("q_stack", [P, NG, HG, TOK], F32R)
        k_stack = sb("k_stack", [P, NG, HG, TOK], F32R)
        v_ones = sb("v_ones", [P, NT, HEADS, 2 * HD])
        probs = sb("probs", [P, 2, HG, TOK])
        neg_max = sb("neg_max", [P, 2, HG * NT])
        max_t = [sb(f"max_t{i}", [HG * NT, P], F32R) for i in "hl"]
        o_raw = sb("o_raw", [P, TOK])
        low_squares = sb("low_squares", [P, 3])
        all_exact = sb("all_exact", [1, 1], I32)
        inv_sum = sb("inv_sum", [P, NT, HG])
        o_norm = sb("o_norm", [P, NT, C])
        gated = sb("gated", [P, TOK])
        hid = sb("hid", [P, 2, TOK])
        hid_t = [sb(f"hid_t{i}", [P, KH, TOK], F32R) for i in "hl"]
        resid = sb("resid", [P, NT, C])
        raw = probs[:, :, :, :].rearrange("p a h n -> p (a h n)")
        raw_qkv = raw[:, 0:KC * 3 * C].rearrange("p (k n) -> p k n", k=KC)
        raw_p = raw[:, KC * 3 * C:KC * 4 * C].rearrange("p (k n) -> p k n", k=KC)
        raw_g = raw[:, KC * 4 * C:KC * 4 * C + KH * C]
        raw_u = v_ones[:, :, :, :].rearrange("p a h n -> p (a h n)")[:, 0:KH * C]
        raw_d = raw[:, 0:KH * C]

        st_bank = [ps(f"st_bank{i}", [P, TOK]) for i in range(2)]
        s_bank = [ps(f"s_bank{i}", [P, TOK]) for i in range(2)]
        o_bank = ps("o_bank", [P, TOK])
        dense = [ps(f"dense{i}", [P, TOK]) for i in range(DENSE_BANKS)]

        w_in = [sem(f"w_in_{n}") for n in ("qkv", "p", "g", "u", "d")]
        bias_in = sem("bias_in")
        x_in = sem("x_in")
        resid_in = sem("resid_in")
        spread = [sem(f"spread{i}") for i in range(2)]
        stack_in = [sem(f"stack_in{g}") for g in range(NG)]
        max_in = [sem(f"max_in{g}") for g in range(NG)]
        out_done = sem("out_done")
        ident_zero = sem("ident_zero")
        ident_ready = sem("ident_ready")
        const_pool = sem("const_pool")
        w_high = sem("w_high")
        w_low = sem("w_low")
        w_float = sem("w_float")
        squares_done = sem("squares_done")
        squares_sum = sem("squares_sum")
        exact_known = sem("exact_known")
        st_done = sem("st_done")
        exp_done = sem("exp_done")
        s_done = sem("s_done")
        max_done = sem("max_done")
        pv_done = sem("pv_done")
        o_raw_done = sem("o_raw_done")
        inv_done = sem("inv_done")
        dense_done = sem("dense_done")
        act_done = sem("act_done")
        dense_free = sem("dense_free")
        hid_high = sem("hid_high")
        hid_low = sem("hid_low")
        stats_done = sem("stats_done")
        moments_done = sem("moments_done")
        var_done = sem("var_done")
        rstd_done = sem("rstd_done")
        xn_done = sem("xn_done")
        resid_ready = sem("resid_ready")

        block = ctx.enter_context(nc.Block())

        def bank_of(row, chunk):
            return dense[(count(Row(row.like, row.like), ALL, chunk) - 1) % DENSE_BANKS]

        def place(row, chunk):
            if row.like == -1 and CHUNKS.index(chunk) < CHUNKS.index(FIRST_MAXIMA):
                return min(chunk[:2], (STEPS - LEAD - 1, 3))
            if row.like == -1 and chunk == FIRST_MAXIMA:
                return STEPS - LEAD + HG, 0
            return chunk[:2]

        def chunks_at(row, step, slot):
            return [c for c in CHUNKS if row.exists(c) and place(row, c) == (step, slot)]

        def head_ahead(row, step):
            s = step + LEAD
            if not 0 <= STEPS * row.like + s < STEPS * ROWS:
                return None
            return s % STEPS // HG, s % HG, STEPS * row.at + s, s // STEPS

        def of_row(row, offset):
            return Row(row.at + offset, row.like + offset)

        def weight_place(kind, i):
            w = {"wgate": w_g, "wup": w_u, "wdown": w_d}[kind]
            if kind == "wdown":
                return w, (slice(None), slice(2 * i, 2 * i + 2), slice(None))
            return w, (slice(None), slice(None), slice(C * i, C * (i + 1)))

        @block.sync
        def _(sp):
            def load_x(at):
                sp.dma_start(xn[:, :, :], x_rows[at]).then_inc(x_in, 16)

            def raw_weight(n, dst, src):
                sp.dma_start(dst, src).then_inc(w_in[n], 16)

            def spread_heads(row, i):
                sp.wait_ge(dense_free, count(row, ALL, kind="k", index=i))
                heads = slice(2 * HG * i, 2 * HG * (i + 1))
                for part in range(2):
                    sp.dma_start(q_spread[heads, part], qk_parts[:, 0, part, :].bitcast(F32)).then_inc(spread[i], 16)
                for part, half in ((0, 0), (1, 1), (2, 0)):
                    sp.dma_start(k_spread[heads, part], qk_parts[:, 1, half, :].bitcast(F32))\
                      .then_inc(spread[i], 16)

            def heads_spread(row, i):
                sp.wait_ge(spread[i], 80 * (row.at + 2))

            def load_stack(row, g):
                if row.has(0) and g > 0:
                    sp.wait_ge(st_done, 64 * row.at + 16 * (g + 1))
                heads = slice(HG * g, HG * (g + 1))
                for half in range(2):
                    rows = slice(2 * HD * half, 2 * HD * (half + 1))
                    sp.dma_start(q_stack[rows, g].bitcast(F32), q_spread[heads].rearrange("h a d n -> (a d) h n"))\
                      .then_inc(stack_in[g], 16)
                    sp.dma_start(k_stack[rows, g].bitcast(F32),
                                 k_spread[heads, half:half + 2].rearrange("h a d n -> (a d) h n"))\
                      .then_inc(stack_in[g], 16)

            def load_max(row, g, meanwhile=None):
                sp.wait_ge(dense_free, count(row, ALL, kind="max", index=g))
                for part in range(2):
                    at = ONES_ROW + part
                    if meanwhile is not None and part == 1:
                        heads_spread(row, meanwhile)
                    sp.dma_start(q_stack[at:at + 1, g].bitcast(F32), max_t[part][:, :].bitcast(F32))\
                      .then_inc(max_in[g], 16)

            def step(row):
                if row.like == -1:
                    load_x(0)
                    raw_weight(0, raw_qkv, qkv_w.rearrange("(k p) n -> p k n", p=P))
                    sp.dma_start(qk_bias[:, :], qkv_b[0:2 * C].rearrange("(k p) -> p k", p=P),
                                 allow_slow_non_contiguous=True).then_inc(bias_in, 16)
                    sp.dma_start(v_bias[:, :], qkv_b[2 * C:3 * C].partition_broadcast(P)).then_inc(bias_in, 16)
                    sp.dma_start(p_bias[:, :], proj_b.partition_broadcast(P)).then_inc(bias_in, 16)
                    raw_weight(1, raw_p, proj_w.rearrange("(k p) n -> p k n", p=P))
                    raw_weight(2, raw_g.bitcast(I32).rearrange("p (k n) -> p k n", n=C),
                               w_gate.rearrange("(k p) n -> p k n", p=P))
                    raw_weight(3, raw_u.bitcast(I32).rearrange("p (k n) -> p k n", n=C),
                               w_up.rearrange("(k p) n -> p k n", p=P))
                    sp.wait_ge(w_high, 2)
                    sp.wait_ge(w_low, 2)
                    raw_weight(4, raw_d.bitcast(I32).rearrange("p (k n) -> p k n", n=HID),
                               w_down.rearrange("(k p) n -> p k n", p=P))
                if row.has(0):
                    if row.has(1):
                        sp.wait_ge(dense_done, count(of_row(row, -1), ALL, kind="xn", index=1))
                        load_x(row.at + 1)
                    load_max(row, 1)
                if row.has(-1):
                    sp.wait_ge(dense_free, count(row, ALL, kind="proj", index=1))
                    sp.dma_start(out_rows[row.at - 1], resid[:, :, :]).then_inc(out_done, 16)
                    sp.wait_ge(out_done, 16 * row.at)
                if row.has(0):
                    sp.dma_start(resid[:, :, :], x_rows[row.at]).then_inc(resid_in, 16)
                    load_max(row, 2)
                if row.has(1):
                    spread_heads(row, 0)
                    heads_spread(row, 0)
                    load_stack(row, 0)
                    load_stack(row, 1)
                    spread_heads(row, 1)
                if row.has(0):
                    load_max(row, 3, meanwhile=1 if row.has(1) else None)
                elif row.has(1):
                    heads_spread(row, 1)
                if row.has(1):
                    load_stack(row, 2)
                    load_max(row, 0)
                    load_stack(row, 3)

            rows_of(sp, step)

        @block.gpsimd
        def _(pool):
            nc.gpsimd.memset(ident[:, :], 0.0).then_inc(ident_zero, 1)
            pool.wait_ge(ident_zero, 1)
            nc.gpsimd.affine_select(out=ident[:, :], in_=ident[:, :], compare_op=ALU.not_equal, fill=1.0, base=0,
                                    pattern=[[-1, P]], channel_multiplier=1).then_inc(ident_ready, 1)
            nc.gpsimd.memset(minus_half[:, :], -0.5)
            nc.gpsimd.memset(eps[:, :], EPS).then_inc(const_pool, 1)
            pool.wait_ge(const_pool, 1)

            def deviation(row):
                n = row.at + 1
                pool.wait_ge(moments_done, NT * (n + 1))
                nc.gpsimd.tensor_tensor(rstd[:, :], moments[:, :, 1], eps[:, :], ALU.add).then_inc(var_done, 1)
                pool.wait_ge(var_done, n + 1)
                nc.gpsimd.tensor_tensor(rstd[:, :], rstd[:, :], minus_half[:, :], ALU.pow).then_inc(rstd_done, 1)

            def hidden_low(row, chunk):
                n = count(row, ("up",), chunk)
                pool.wait_ge(dense_free, count(row, ALL, chunk))
                pool.wait_ge(hid_high, n)
                m = chunk[3]
                nc.gpsimd.tensor_tensor(hid_t[1][:, m, :], hid[:, m % 2, :], hid_t[0][:, m, :].bitcast(F32),
                                        ALU.subtract).then_inc(hid_low, 1)

            def step(row):
                if row.like == -1:
                    deviation(row)
                    pool.wait_ge(rstd_done, 1)
                    for g in range(NG):
                        nc.gpsimd.memset(k_stack[64:P, g].bitcast(F32), 1.0).then_inc(const_pool, 1)
                        pool.wait_ge(const_pool, 2 * g + 2)
                        nc.gpsimd.memset(q_stack[64:ONES_ROW, g].bitcast(F32), 0.0).then_inc(const_pool, 1)
                        pool.wait_ge(const_pool, 2 * g + 3)
                for s in range(STEPS):
                    if s == AVERAGE_AT // 4 and row.has(1) and row.like >= 0:
                        deviation(row)
                    if s == 9 and row.like == -1:
                        pool.wait_ge(dense_done, count(row, ALL, kind="wup", index=2))
                        nc.gpsimd.memset(v_ones[:, :, :, :], 1.0).then_inc(const_pool, 1)
                    if s == 5 and row.has(0):
                        pool.wait_ge(resid_in, 16 * (row.at + 1))
                        pool.wait_ge(bias_in, 48)
                        for t in range(NT):
                            nc.gpsimd.tensor_tensor(resid[:, t, :], resid[:, t, :], p_bias[:, :],
                                                    ALU.add).then_inc(resid_ready, 1)
                    for slot in range(4):
                        for chunk in chunks_at(row, s, slot):
                            if chunk[2] == "up":
                                hidden_low(row, chunk)

            rows_of(pool, step)

        @block.scalar
        def _(act):
            def split_high(n, dst, src):
                act.wait_ge(w_in[n], 16)
                nc.scalar.activation(dst, src, ACT.Copy).then_inc(w_high, 1)

            def exp(row, s, j):
                tile = 64 * row.at + 4 * s + j
                act.wait_ge(st_done, tile + 1)
                if j == 0 and 16 * row.like + s >= 2:
                    act.wait_ge(pv_done, 16 * row.at + s - 1)
                if row.like == 0 and s < 2:
                    act.wait_ge(squares_done, 3)
                nc.scalar.activation(probs[:, s % 2, j, :], st_bank[j % 2][:, :], ACT.Exp,
                                     scale=SCALE).then_inc(exp_done, 1)

            def take(row, chunk):
                _, _, kind, i, _ = chunk
                bank = bank_of(row, chunk)
                act.wait_ge(dense_done, count(row, ALL, chunk))
                if kind == "xn":
                    nc.scalar.activation(xn_t[0][:, i, :], bank[:, :], ACT.Copy).then_inc(act_done, 1)
                elif kind in ("q", "k"):
                    which = 0 if kind == "q" else 1
                    if row.has(0) or i == 1:
                        act.wait_ge(spread[1 - i], 80 * (row.at + 1 + i))
                    act.wait_ge(bias_in, 48)
                    nc.scalar.activation(qk_parts[:, which, 0, :], bank[:, :], ACT.Identity,
                                         bias=qk_bias[:, KC * which + i:KC * which + i + 1]).then_inc(act_done, 1)
                elif kind == "max":
                    g = 4 * (row.at + chunk[4]) + i
                    if 4 * (row.like + chunk[4]) + i >= 1:
                        act.wait_ge(max_in[(i - 1) % NG], 32 * (row.at + (1 if i else 0) + chunk[4]))
                    nc.scalar.activation(max_t[0][:, :], bank[0:HG * NT, 0:P], ACT.Copy).then_inc(act_done, 1)
                elif kind == "ot":
                    if i == 0:
                        act.wait_ge(spread[1], 80 * (row.at + (1 if row.has(0) else 0)))
                    nc.scalar.activation(qk_parts[:, i, 0, :], bank[:, :], ACT.Copy).then_inc(act_done, 1)
                elif kind == "gate":
                    if not (row.like == -1 and i == 0):
                        act.wait_ge(dense_free, count(row, ALL, chunk) - 1)
                    nc.scalar.activation(gated[:, :], bank[:, :], ACT.Tanh, scale=0.5 * QUANT).then_inc(act_done, 1)
                else:
                    w, cols = weight_place(kind, i)
                    nc.scalar.activation(w[0][cols], bank[:, :].rearrange("p (a n) -> p a n", a=2),
                                         ACT.Copy).then_inc(act_done, 1)

            def square_lows():
                act.wait_ge(dense_free, count(Row(-1, -1), ALL, kind="wdown", index=2))
                for n, w in enumerate((w_g, w_u, w_d)):
                    if n:
                        act.wait_ge(squares_done, n)
                    low = w[1][:, :, :].rearrange("p k n -> p (k n)").bitcast(F32)
                    nc.scalar.activation(raw[:, 0:KH * C], low, ACT.Square,
                                         accum_out=low_squares[:, n:n + 1]).then_inc(squares_done, 1)

            def hidden_high(row, chunk):
                act.wait_ge(dense_free, count(row, ALL, chunk))
                m = chunk[3]
                nc.scalar.activation(hid_t[0][:, m, :], hid[:, m % 2, :], ACT.Copy).then_inc(hid_high, 1)

            def step(row):
                if row.like == -1:
                    split_high(0, w_qkv[0][:, :, 0:C], raw_qkv[:, :, 0:C])
                    split_high(0, w_qkv[0][:, :, C:3 * C], raw_qkv[:, :, C:3 * C])
                    split_high(1, w_p[0][:, :, :], raw_p)
                for s in range(STEPS):
                    for slot in range(4):
                        if row.has(0):
                            exp(row, s, slot)
                        for r in (of_row(row, -1), row):
                            before = STEPS * 4 * (row.like - r.like) + 4 * s + slot - HIGH_DELAY
                            for chunk in CHUNKS:
                                if chunk[2] == "up" and r.like >= 0 and r.exists(chunk) and 4 * chunk[0] + chunk[1] == before:
                                    hidden_high(r, chunk)
                        for chunk in chunks_at(row, s, slot):
                            if chunk[2] in ON_ACT:
                                take(row, chunk)
                            if row.like == -1 and chunk[2] == "up":
                                hidden_high(row, chunk)
                            if row.like == -1 and chunk[2:4] == SQUARES_AFTER:
                                square_lows()
                        if slot == O_SLOT and s % NT == 0 and 0 < 16 * row.like + s <= 16 * ROWS:
                            act.wait_ge(pv_done, 16 * row.at + s)
                            if 16 * row.like + s > 4:
                                g = (s // NT - 2) % NG
                                shift = -1 if s == 0 else 0
                                act.wait_ge(dense_done, count(of_row(row, shift), ALL, kind="o", index=g))
                            nc.scalar.activation(o_raw[:, :], o_bank[:, :], ACT.Copy).then_inc(o_raw_done, 1)

            rows_of(act, step)

        @block.vector
        def _(dve):
            def statistics(row, t):
                if t == 0:
                    dve.wait_ge(x_in, 16 * (row.at + 2))
                nc.vector.bn_stats(stats[:, t, :], xn[:, t, :]).then_inc(stats_done, 1)

            def statistics_done(row):
                dve.wait_ge(stats_done, NT * (row.at + 2))

            def average():
                for t in range(NT):
                    nc.vector.bn_aggr(moments[:, t, :], stats[:, t, :]).then_inc(moments_done, 1)

            def normalise(row, t):
                if t == 0:
                    dve.wait_ge(rstd_done, row.at + 2)
                nc.vector.tensor_scalar(xn[:, t, :], xn[:, t, :], moments[:, t, 0:1], rstd[:, t:t + 1],
                                        ALU.subtract, ALU.mult).then_inc(xn_done, 1)

            def maximum(row, s, q):
                g, h, item, ahead = head_ahead(row, s)
                dve.wait_ge(s_done, 4 * item + q + 1)
                nc.vector.tensor_reduce(neg_max[:, g % 2, NT * h + q:NT * h + q + 1], s_bank[q % 2][:, :], AX_X,
                                        ALU.max, negate=True).then_inc(max_done, 1)

            def take(row, chunk):
                _, _, kind, i, offset = chunk
                bank = bank_of(row, chunk)
                if kind in ON_ACT:
                    dve.wait_ge(act_done, count(row, ON_ACT, chunk))
                else:
                    dve.wait_ge(dense_done, count(row, ALL, chunk))
                if kind == "xn":
                    nc.vector.tensor_tensor(xn_t[1][:, i, :], bank[:, :], xn_t[0][:, i, :].bitcast(F32),
                                            ALU.subtract).then_inc(dense_free, 1)
                elif kind in ("q", "k"):
                    which = 0 if kind == "q" else 1
                    nc.vector.scalar_tensor_tensor(qk_parts[:, which, 1, :], bank[:, :],
                                                   qk_bias[:, KC * which + i:KC * which + i + 1],
                                                   qk_parts[:, which, 0, :].bitcast(F32),
                                                   ALU.add, ALU.subtract).then_inc(dense_free, 1)
                elif kind == "v":
                    if i == 0 and row.has(-1):
                        dve.wait_ge(pv_done, 16 * row.at)
                    if i == 0 and row.like == 0:
                        dve.wait_ge(const_pool, 2 * NG + 2)
                        dve.wait_ge(bias_in, 48)
                    for u in range(2):
                        done = nc.vector.tensor_tensor(v_ones[:, 2 * i + u, :, 0:HD],
                                                       bank[:, C * u:C * (u + 1)].rearrange("p (h d) -> p h d", d=HD),
                                                       v_bias[:, :].rearrange("p (h d) -> p h d", d=HD), ALU.add)
                    done.then_inc(dense_free, 1)
                elif kind == "max":
                    nc.vector.tensor_tensor(max_t[1][:, :], bank[0:HG * NT, 0:P], max_t[0][:, :].bitcast(F32),
                                            ALU.subtract).then_inc(dense_free, 1)
                elif kind == "o":
                    heads = bank[:, :].rearrange("p (t h d) -> p t h d", t=NT, h=HG)
                    if 4 * (row.like + offset) + i >= 1:
                        dve.wait_ge(dense_free, count(row, ALL, chunk) - 1)
                    nc.vector.reciprocal(inv_sum[:, :, :], heads[:, :, :, HD]).then_inc(inv_done, 1)
                    dve.wait_ge(inv_done, 4 * (row.at + offset) + i + 1)
                    nc.vector.tensor_tensor(
                        o_norm[:, :, HG * HD * i:HG * HD * (i + 1)].rearrange("p t (h d) -> p t h d", d=HD),
                        heads[:, :, :, 0:HD], inv_sum[:, :, :].unsqueeze(3).broadcast_to([P, NT, HG, HD]),
                        ALU.mult).then_inc(dense_free, 1)
                elif kind == "ot":
                    nc.vector.tensor_tensor(qk_parts[:, i, 1, :], bank[:, :], qk_parts[:, i, 0, :].bitcast(F32),
                                            ALU.subtract).then_inc(dense_free, 1)
                elif kind == "gate":
                    nc.vector.scalar_tensor_tensor(gated[:, :], gated[:, :], 1.0, bank[:, :], ALU.add,
                                                   ALU.mult).then_inc(dense_free, 1)
                elif kind == "up":
                    n = count(row, ("up",), chunk)
                    if not (row.like == -1 and i < 2):
                        dve.wait_ge(hid_high, n - 2)
                        dve.wait_ge(hid_low, n - 2)
                    dve.wait_ge(dense_free, count(row, ALL, chunk) - 1)
                    nc.vector.scalar_tensor_tensor(hid[:, i % 2, :], bank[:, :], 0.5 * QUANT ** 3, gated[:, :],
                                                   ALU.mult, ALU.mult).then_inc(dense_free, 1)
                elif kind == "down":
                    if i == 0:
                        dve.wait_ge(resid_ready, NT * (row.at + 1))
                    nc.vector.tensor_tensor(resid[:, i, :], bank[:, 0:C], resid[:, i, :],
                                            ALU.add).then_inc(dense_free, 1)
                elif kind == "proj":
                    if i == 0:
                        dve.wait_ge(dense_free, count(of_row(row, -1), ALL, kind="down", index=3))
                    both = resid[:, 2 * i:2 * i + 2, :]
                    nc.vector.tensor_tensor(both, bank[:, :].rearrange("p (t n) -> p t n", t=2), both,
                                            ALU.add).then_inc(dense_free, 1)
                else:
                    w, cols = weight_place(kind, i)
                    nc.vector.tensor_tensor(w[1][cols],
                                            bank[:, :].rearrange("p (a n) -> p a n", a=2),
                                            w[0][cols].bitcast(F32), ALU.subtract).then_inc(dense_free, 1)

            def split_low(n, dst, src, high):
                dve.wait_ge(w_high, n)
                nc.vector.tensor_tensor(dst, src, high.bitcast(F32), ALU.subtract).then_inc(w_low, 1)

            def to_float(n, ints):
                dve.wait_ge(w_in[n], 16)
                nc.vector.tensor_copy(ints, ints.bitcast(I32)).then_inc(w_float, 1)

            def decide():
                dve.wait_ge(squares_sum, 1)
                nc.vector.tensor_scalar(all_exact[:, :], o_bank[0:1, 0:1], 0.0, None,
                                        ALU.is_equal).then_inc(exact_known, 1)

            def step(row):
                if row.like == -1:
                    for t in range(NT):
                        statistics(row, t)
                    statistics_done(row)
                    average()
                    for t in range(NT):
                        normalise(row, t)
                    split_low(1, w_qkv[1][:, :, 0:C], raw_qkv[:, :, 0:C], w_qkv[0][:, :, 0:C])
                    split_low(2, w_qkv[1][:, :, C:3 * C], raw_qkv[:, :, C:3 * C], w_qkv[0][:, :, C:3 * C])
                for s in range(STEPS):
                    for slot in range(4):
                        at = 4 * s + slot
                        layernorm = row.like >= 0 and row.has(1)
                        if layernorm and 0 <= at - STATS_AT < NT:
                            statistics(row, at - STATS_AT)
                        if layernorm and 0 <= at - NORMALISE_AT < NT:
                            normalise(row, at - NORMALISE_AT)
                        if layernorm and at == AVERAGE_AT:
                            statistics_done(row)
                        if head_ahead(row, s):
                            maximum(row, s, slot)
                        if layernorm and at == AVERAGE_AT:
                            average()
                        for chunk in chunks_at(row, s, slot):
                            take(row, chunk)
                            if row.like == -1:
                                if chunk[2:4] == ("xn", 1):
                                    to_float(2, raw_g)
                                    to_float(3, raw_u)
                                elif chunk[2:4] == ("k", 0):
                                    to_float(4, raw_d)
                                    split_low(3, w_p[1][:, :, :], raw_p, w_p[0][:, :, :])
                                elif chunk[2:4] == DECISION_AFTER:
                                    decide()

            rows_of(dve, step)

        @block.tensor
        def _(pe):
            SPLIT = ((0, 0), (1, 0), (0, 1))
            STATIONARY_EXACT = ((0, 0), (0, 1))
            MOVING_EXACT = ((0, 0), (1, 0))

            def scores_t(row, s, j):
                g, kt = s // NT, s % NT
                tile = 64 * row.at + 4 * s + j
                if kt == 0 and j == 0:
                    pe.wait_ge(max_in[g], 32 * (row.at + 1))
                if 16 * row.like + s > 0 or j >= 2:
                    pe.wait_ge(exp_done, tile - 1)
                nc.tensor.matmul(st_bank[j % 2][:, :], k_stack[0:STACK, g, j, P * kt:P * (kt + 1)],
                                 q_stack[0:STACK, g, j, :], start=True, stop=True).then_inc(st_done, 1)

            def scores(row, s, q):
                g, h, item, ahead = head_ahead(row, s)
                if h == 0 and q == 0:
                    pe.wait_ge(stack_in[g], 64 * (row.at + ahead + 1))
                    if row.like + ahead == 0:
                        pe.wait_ge(const_pool, 2 * g + 3)
                if 16 * row.like + s + LEAD > 0 or q >= 2:
                    pe.wait_ge(max_done, 4 * item + q - 1)
                nc.tensor.matmul(s_bank[q % 2][:, :], q_stack[0:ONES_ROW, g, h, P * q:P * (q + 1)],
                                 k_stack[0:ONES_ROW, g, h, :], start=True, stop=True).then_inc(s_done, 1)

            def probs_v(row, s):
                g, kt = (s - 1) % STEPS // NT, (s - 1) % NT
                n = 16 * row.at + s
                pe.wait_ge(exp_done, 4 * n)
                if s == 1:
                    pe.wait_ge(dense_free, count(row, ALL, kind="v", index=1))
                if kt == 0 and 16 * row.like + s > 1:
                    pe.wait_ge(o_raw_done, 4 * row.at + s // NT)
                for j in range(HG):
                    done = nc.tensor.matmul(o_bank[32 * j:32 * (j + 1), :], v_ones[:, kt, HG * g + j, :],
                                            probs[:, (s - 1) % 2, j, :], start=kt == 0, stop=kt == NT - 1,
                                            tile_position=(0, 32 * j))
                done.then_inc(pv_done, 1)

            def product(bank, stationary, moving, tiles, parts=SPLIT):
                for n, (a, b) in enumerate(parts):
                    for k in range(tiles):
                        done = nc.tensor.matmul(bank, stationary(a, k), moving(b, k), start=n == 0 and k == 0,
                                                stop=n == len(parts) - 1 and k == tiles - 1)
                return done

            def chunk_products(row, chunk, exact):
                _, _, kind, i, offset = chunk
                bank = bank_of(row, chunk)
                n = count(row, ALL, chunk)
                if count(Row(row.like, row.like), ALL, chunk) > DENSE_BANKS:
                    pe.wait_ge(dense_free, n - DENSE_BANKS)
                if kind == "xn":
                    if i == 0:
                        pe.wait_ge(xn_done, NT * (row.at + 2))
                    for t in range(NT):
                        done = nc.tensor.transpose(bank[:, P * t:P * (t + 1)], xn[:, t, P * i:P * (i + 1)], ident[:, :])
                elif kind in ("q", "k"):
                    if kind == "q" and i == 0:
                        pe.wait_ge(dense_free, count(row, ALL, kind="xn", index=1))
                        if row.like == -1:
                            pe.wait_ge(w_low, 2)
                    base = (0 if kind == "q" else C) + P * i
                    done = product(bank[:, :], lambda a, k: w_qkv[a][:, k, base:base + P],
                                   lambda b, k: xn_t[b][:, k, :], KC)
                elif kind == "v":
                    for u in range(2):
                        t = 2 * i + u
                        done = product(bank[:, C * u:C * (u + 1)], lambda a, k: xn_t[a][:, k, P * t:P * (t + 1)],
                                       lambda b, k: w_qkv[b][:, k, 2 * C:3 * C], KC)
                elif kind == "max":
                    pe.wait_ge(max_done, 16 * (4 * (row.at + offset) + i + 1))
                    done = nc.tensor.transpose(bank[0:HG * NT, 0:P], neg_max[:, i % 2, :], ident[:, :])
                elif kind == "o":
                    pe.wait_ge(o_raw_done, 4 * (row.at + offset) + i + 1)
                    for t in range(NT):
                        done = nc.tensor.transpose(bank[:, P * t:P * (t + 1)], o_raw[:, P * t:P * (t + 1)], ident[:, :])
                elif kind == "ot":
                    if i == 0:
                        pe.wait_ge(dense_free, count(row, ALL, kind="o", index=3))
                    for t in range(NT):
                        done = nc.tensor.transpose(bank[:, P * t:P * (t + 1)], o_norm[:, t, P * i:P * (i + 1)], ident[:, :])
                elif kind in ("gate", "up"):
                    w = w_g if kind == "gate" else w_u
                    if row.like == -1 and i == 0:
                        pe.wait_ge(dense_free, count(row, ALL, kind="wdown", index=2))
                    done = product(bank[:, :], lambda a, k: w[a][:, k, P * i:P * (i + 1)],
                                   lambda b, k: xn_t[b][:, k, :], KC, STATIONARY_EXACT if exact else SPLIT)
                elif kind == "down":
                    if i == 0:
                        pe.wait_ge(hid_high, KH * (row.at + 1))
                        pe.wait_ge(hid_low, KH * (row.at + 1))
                    done = product(bank[:, 0:C], lambda a, k: hid_t[a][:, k, P * i:P * (i + 1)],
                                   lambda b, k: w_d[b][:, k, :], KH, MOVING_EXACT if exact else SPLIT)
                elif kind == "proj":
                    if i == 0:
                        pe.wait_ge(dense_free, count(row, ALL, kind="ot", index=1))
                    for u in range(2):
                        t = 2 * i + u
                        done = product(bank[:, C * u:C * (u + 1)], lambda a, k: qk_parts[:, k, a, P * t:P * (t + 1)],
                                       lambda b, k: w_p[b][:, k, :], KC)
                elif kind == "wdown":
                    pe.wait_ge(w_float, 3)
                    d = raw_d.rearrange("p (k n) -> p k n", n=HID)
                    for t in range(4):
                        m, c = 2 * i + t // 2, t % 2
                        done = nc.tensor.transpose(bank[:, P * t:P * (t + 1)], d[:, c, P * m:P * (m + 1)], ident[:, :])
                else:
                    pe.wait_ge(w_float, 1 if kind == "wgate" else 2)
                    w = (raw_g if kind == "wgate" else raw_u).rearrange("p (k n) -> p k n", n=C)
                    for t in range(4):
                        c, m = t // 2, 2 * i + t % 2
                        done = nc.tensor.transpose(bank[:, P * t:P * (t + 1)], w[:, m, P * c:P * (c + 1)], ident[:, :])
                done.then_inc(dense_done, 1)

            def sum_squares():
                pe.wait_ge(squares_done, 3)
                for n in range(3):
                    done = nc.tensor.matmul(o_bank[0:1, 0:1], minus_half[:, 0:1], low_squares[:, n:n + 1],
                                            start=n == 0, stop=n == 2)
                done.then_inc(squares_sum, 1)

            def step(row, exact):
                for s in range(STEPS):
                    for slot in range(4):
                        if row.has(0):
                            scores_t(row, s, slot)
                        if slot == PV_SLOT and 0 < 16 * row.like + s <= 16 * ROWS:
                            probs_v(row, s)
                        if row.like == -1 and head_ahead(row, s):
                            scores(row, s, slot)
                        for chunk in chunks_at(row, s, slot):
                            chunk_products(row, chunk, exact)
                            if row.like == -1 and chunk[2:4] == DECISION_AFTER:
                                sum_squares()
                        if row.like >= 0 and head_ahead(row, s):
                            scores(row, s, slot)

            def rows_from_0(exact):
                step(Row(0, 0), exact)
                with pe.Fori(1, ROWS - 1) as b:
                    step(Row(b, 1), exact)
                step(Row(ROWS - 1, ROWS - 1), exact)
                step(Row(ROWS, ROWS), exact)

            pe.wait_ge(ident_ready, 1)
            step(Row(-1, -1), False)
            pe.wait_ge(exact_known, 1)
            flag = pe.value_load(all_exact[0:1, 0:1], min_val=0, max_val=1)
            with pe.If(flag == 1):
                rows_from_0(True)
            with pe.Else():
                rows_from_0(False)


_INS = ["L0_attn_x", "L0_attn_qkv_w", "L0_attn_qkv_b", "L0_attn_proj_w", "L0_attn_proj_b",
        "L0_ffn_w_gate", "L0_ffn_w_up", "L0_ffn_w_down"]


def kernel(**inputs):
    import numpy as _np
    import concourse.bacc as _bacc
    from concourse import mybir as _mybir
    from concourse.bass_utils import run_bass_kernel_spmd as _run

    nc = _bacc.Bacc("TRN2", target_bir_lowering=False, num_devices=1)
    arrays, args = {}, []
    for name in _INS:
        a = _np.ascontiguousarray(inputs[name])
        arrays[f"in_{name}"] = a
        args.append(nc.dram_tensor(f"in_{name}", a.shape, _mybir.dt.from_np(a.dtype), kind="ExternalInput").ap())
    out = nc.dram_tensor("out_0", (ROWS, TOK, C), F32, kind="ExternalOutput").ap()
    build(nc, *args, out)
    r = _run(nc, [arrays], core_ids=[0])
    return r.results[0]["out_0"]
```

```python
from contextlib import ExitStack

import concourse.bass as bass
from concourse import mybir

F32 = mybir.dt.float32
F32R = mybir.dt.float32r
I32 = mybir.dt.int32
ALU = mybir.AluOpType
ACT = mybir.ActivationFunctionType
AX_X = mybir.AxisListType.X

P = 128
ROWS = 8
TOK = 512
NT = TOK // P
C = 256
KC = C // P
HEADS = 16
HD = C // HEADS
HG = 4
NG = HEADS // HG
HID = 768
KH = HID // P
STEPS = NG * NT
LEAD = 6
SCALE = float(HD) ** -0.5
QUANT = 1.0 / 127.0
EPS = 1e-5
ONES_ROW = 96
STACK = ONES_ROW + 2
DENSE_BANKS = 3
WARM_UP = 8
BUSY_AFTER = {"last": 4, ("o", 3): 4, ("ot", 1): 4}
PV_SLOT = 2
O_SLOT = 2
STATS_AT = 11
AVERAGE_AT = 14
NORMALISE_AT = 18
HIGH_DELAY = 3

WPREP = ("wgate", "wup", "wdown")
CHUNKS = [
    (0, 0, "v", 0, 0), (0, 3, "v", 1, 0),
    (1, 0, "gate", 3, 0), (1, 2, "o", 3, -1),
    (2, 0, "up", 3, 0), (2, 1, "ot", 0, -1), (2, 1, "max", 1, 0), (2, 2, "ot", 1, -1),
    (3, 1, "proj", 0, -1), (3, 3, "proj", 1, -1),
    (4, 1, "gate", 4, 0), (4, 3, "up", 4, 0),
    (5, 0, "gate", 5, 0), (5, 1, "up", 5, 0), (5, 3, "xn", 0, 1),
    (6, 0, "xn", 1, 1), (6, 0, "o", 0, 0), (6, 1, "max", 2, 0), (6, 3, "q", 0, 1),
    (7, 0, "k", 0, 1),
] + [(7, 3, w, i, None) for w in WPREP for i in range(3)] + [
    (7, 3, "down", 0, 0),
    (8, 1, "q", 1, 1), (8, 1, "down", 1, 0), (8, 3, "k", 1, 1),
    (9, 0, "down", 2, 0), (9, 3, "o", 1, 0),
    (10, 1, "down", 3, 0), (10, 1, "max", 3, 0),
    (11, 0, "gate", 0, 1),
    (12, 0, "up", 0, 1), (12, 3, "gate", 1, 1),
    (13, 1, "up", 1, 1),
    (14, 0, "o", 2, 0), (14, 1, "max", 0, 1), (14, 3, "gate", 2, 1),
    (15, 1, "up", 2, 1),
]
ON_ACT = ("xn", "q", "k", "max", "ot", "gate") + WPREP
FIRST_MAXIMA = next(c for c in CHUNKS if c[2:] == ("max", 0, 1))
SQUARES_AFTER = ("up", 1)
DECISION_AFTER = ("max", 0)
PROLOGUE = {("gate", 2): (15, 3), ("up", 2): (15, 3), ("gate", 1): (10, 3), ("up", 1): (11, 3)}
ALL = tuple({kind for _, _, kind, _, _ in CHUNKS})


class Row:

    def __init__(self, at, like):
        self.at, self.like = at, like

    def has(self, offset):
        return 0 <= self.like + offset < ROWS

    def exists(self, chunk):
        return self.like == -1 if chunk[4] is None else self.has(chunk[4])


def rows_of(engine, step):
    step(Row(-1, -1))
    step(Row(0, 0))
    with engine.Fori(1, ROWS - 1) as b:
        step(Row(b, 1))
    step(Row(ROWS - 1, ROWS - 1))
    step(Row(ROWS, ROWS))


def count(row, kinds, chunk=None, kind=None, index=None):
    like = row.like
    if chunk is None:
        (chunk,) = [c for c in CHUNKS if c[2] == kind and c[3] == index]
    last = CHUNKS.index(chunk)
    total = 0
    for r in range(-1, like + 1):
        for n, c in enumerate(CHUNKS):
            if c[2] in kinds and Row(r, r).exists(c) and (r < like or n <= last):
                total += 1
    per = sum(c[2] in kinds and c[4] is not None for c in CHUNKS)
    return total + per * (row.at - row.like)


def build(nc, x, qkv_w, qkv_b, proj_w, proj_b, w_gate, w_up, w_down, out):
    x_rows = x.rearrange("b (t p) c -> b p t c", p=P)
    out_rows = out.rearrange("b (t p) c -> b p t c", p=P)
    q_spread = nc.dram_tensor("q_spread", [HEADS, 2, HD, TOK], F32, kind="Internal").ap()
    k_spread = nc.dram_tensor("k_spread", [HEADS, 3, HD, TOK], F32, kind="Internal").ap()

    with ExitStack() as ctx:
        def sb(name, shape, dt=F32):
            return ctx.enter_context(nc.sbuf_tensor(name, shape, dt))

        def ps(name, shape):
            return ctx.enter_context(nc.psum_tensor(name, shape, F32))

        def sem(name):
            return ctx.enter_context(nc.semaphore(name))

        w_qkv = [sb(f"w_qkv{i}", [P, KC, 3 * C], F32R) for i in "hl"]
        w_g = [sb(f"w_g{i}", [P, KC, HID], F32R) for i in "hl"]
        w_u = [sb(f"w_u{i}", [P, KC, HID], F32R) for i in "hl"]
        w_d = [sb(f"w_d{i}", [P, KH, C], F32R) for i in "hl"]
        w_p = [sb(f"w_p{i}", [P, KC, C], F32R) for i in "hl"]
        qk_bias = sb("qk_bias", [P, 2 * KC])
        v_bias = sb("v_bias", [P, C])
        p_bias = sb("p_bias", [P, C])
        ident = sb("ident", [P, P])
        xn = sb("xn", [P, NT, C])
        stats = sb("stats", [P, NT, 6])
        moments = sb("moments", [P, NT, 2])
        rstd = sb("rstd", [P, NT])
        minus_half = sb("minus_half", [P, NT])
        eps = sb("eps", [P, NT])
        xn_t = [sb(f"xn_t{i}", [P, KC, TOK], F32R) for i in "hl"]
        qk_parts = sb("qk_parts", [P, 2, 2, TOK], F32R)
        q_stack = sb("q_stack", [P, NG, HG, TOK], F32R)
        k_stack = sb("k_stack", [P, NG, HG, TOK], F32R)
        v_ones = sb("v_ones", [P, NT, HEADS, 2 * HD])
        probs = sb("probs", [P, 2, HG, TOK])
        neg_max = sb("neg_max", [P, 2, HG * NT])
        max_t = [sb(f"max_t{i}", [HG * NT, P], F32R) for i in "hl"]
        o_raw = sb("o_raw", [P, TOK])
        low_squares = sb("low_squares", [P, 3])
        all_exact = sb("all_exact", [1, 1], I32)
        inv_sum = sb("inv_sum", [P, NT, HG])
        o_norm = sb("o_norm", [P, NT, C])
        gated = sb("gated", [P, TOK])
        hid = sb("hid", [P, 2, TOK])
        hid_t = [sb(f"hid_t{i}", [P, KH, TOK], F32R) for i in "hl"]
        resid = sb("resid", [P, NT, C])
        raw = probs[:, :, :, :].rearrange("p a h n -> p (a h n)")
        raw_qkv = raw[:, 0:KC * 3 * C].rearrange("p (k n) -> p k n", k=KC)
        raw_p = raw[:, KC * 3 * C:KC * 4 * C].rearrange("p (k n) -> p k n", k=KC)
        raw_g = raw[:, KC * 4 * C:KC * 4 * C + KH * C]
        raw_u = v_ones[:, :, :, :].rearrange("p a h n -> p (a h n)")[:, 0:KH * C]
        raw_d = raw[:, 0:KH * C]

        st_bank = [ps(f"st_bank{i}", [P, TOK]) for i in range(2)]
        s_bank = [ps(f"s_bank{i}", [P, TOK]) for i in range(2)]
        o_bank = ps("o_bank", [P, TOK])
        dense = [ps(f"dense{i}", [P, TOK]) for i in range(DENSE_BANKS)]

        w_in = [sem(f"w_in_{n}") for n in ("qkv", "p", "g", "u", "d")]
        bias_in = sem("bias_in")
        x0_in = [sem(f"x0_in{i}") for i in range(2)]
        x_in = sem("x_in")
        resid_in = sem("resid_in")
        spread = [sem(f"spread{i}") for i in range(2)]
        stack_in = [sem(f"stack_in{g}") for g in range(NG)]
        max_in = [sem(f"max_in{g}") for g in range(NG)]
        out_done = sem("out_done")
        ident_zero = sem("ident_zero")
        ident_ready = sem("ident_ready")
        const_pool = sem("const_pool")
        w_high = sem("w_high")
        w_low = sem("w_low")
        w_float = sem("w_float")
        squares_done = sem("squares_done")
        squares_sum = sem("squares_sum")
        exact_known = sem("exact_known")
        st_done = sem("st_done")
        exp_done = sem("exp_done")
        s_done = sem("s_done")
        max_done = sem("max_done")
        pv_done = sem("pv_done")
        o_raw_done = sem("o_raw_done")
        inv_done = sem("inv_done")
        dense_done = sem("dense_done")
        act_done = sem("act_done")
        dense_free = sem("dense_free")
        hid_high = sem("hid_high")
        hid_low = sem("hid_low")
        stats_done = sem("stats_done")
        moments_done = sem("moments_done")
        var_done = sem("var_done")
        rstd_done = sem("rstd_done")
        xn_done = sem("xn_done")
        resid_ready = sem("resid_ready")

        block = ctx.enter_context(nc.Block())

        def bank_of(row, chunk):
            return dense[(count(Row(row.like, row.like), ALL, chunk) - 1) % DENSE_BANKS]

        def place(row, chunk):
            if row.like == -1 and chunk[2:4] in PROLOGUE:
                return PROLOGUE[chunk[2:4]]
            if row.like == -1 and CHUNKS.index(chunk) < CHUNKS.index(FIRST_MAXIMA):
                return min(chunk[:2], (STEPS - LEAD - 1, 3))
            if row.like == -1 and chunk == FIRST_MAXIMA:
                return STEPS - LEAD + HG, 0
            return chunk[:2]

        def chunks_at(row, step, slot):
            return [c for c in CHUNKS if row.exists(c) and place(row, c) == (step, slot)]

        def head_ahead(row, step):
            s = step + LEAD
            if not 0 <= STEPS * row.like + s < STEPS * ROWS:
                return None
            return s % STEPS // HG, s % HG, STEPS * row.at + s, s // STEPS

        def score_bank(row, q):
            return (s_bank + st_bank)[q] if row.like == -1 else s_bank[q % 2]

        def after_scores(row, step):
            return row.like == ROWS - 1 and step >= STEPS - LEAD

        def transposed_bank(row, step, j):
            return (st_bank + s_bank)[j] if after_scores(row, step) else st_bank[j % 2]

        def of_row(row, offset):
            return Row(row.at + offset, row.like + offset)

        def weight_place(kind, i):
            w = {"wgate": w_g, "wup": w_u, "wdown": w_d}[kind]
            if kind == "wdown":
                return w, (slice(None), slice(2 * i, 2 * i + 2), slice(None))
            return w, (slice(None), slice(None), slice(C * i, C * (i + 1)))

        @block.sync
        def _(sp):
            def load_x(at):
                sp.dma_start(xn[:, :, :], x_rows[at]).then_inc(x_in, 16)

            def raw_weight(n, dst, src):
                sp.dma_start(dst, src).then_inc(w_in[n], 16)

            def spread_heads(row, i):
                sp.wait_ge(dense_free, count(row, ALL, kind="k", index=i))
                heads = slice(2 * HG * i, 2 * HG * (i + 1))
                for part in range(2):
                    sp.dma_start(q_spread[heads, part], qk_parts[:, 0, part, :].bitcast(F32)).then_inc(spread[i], 16)
                for part, half in ((0, 0), (1, 1), (2, 0)):
                    sp.dma_start(k_spread[heads, part], qk_parts[:, 1, half, :].bitcast(F32))\
                      .then_inc(spread[i], 16)

            def heads_spread(row, i):
                sp.wait_ge(spread[i], 80 * (row.at + 2))

            def load_stack(row, g):
                if row.has(0) and g > 0:
                    sp.wait_ge(st_done, 64 * row.at + 16 * (g + 1))
                heads = slice(HG * g, HG * (g + 1))
                for half in range(2):
                    rows = slice(2 * HD * half, 2 * HD * (half + 1))
                    sp.dma_start(q_stack[rows, g].bitcast(F32), q_spread[heads].rearrange("h a d n -> (a d) h n"))\
                      .then_inc(stack_in[g], 16)
                    sp.dma_start(k_stack[rows, g].bitcast(F32),
                                 k_spread[heads, half:half + 2].rearrange("h a d n -> (a d) h n"))\
                      .then_inc(stack_in[g], 16)

            def load_max(row, g, meanwhile=None):
                sp.wait_ge(dense_free, count(row, ALL, kind="max", index=g))
                for part in range(2):
                    at = ONES_ROW + part
                    if meanwhile is not None and part == 1:
                        heads_spread(row, meanwhile)
                    sp.dma_start(q_stack[at:at + 1, g].bitcast(F32), max_t[part][:, :].bitcast(F32))\
                      .then_inc(max_in[g], 16)

            def step(row):
                if row.like == -1:
                    for half in range(2):
                        tiles = slice(half * NT // 2, (half + 1) * NT // 2)
                        sp.dma_start(xn[:, tiles, :], x_rows[0, :, tiles]).then_inc(x0_in[half], 16)
                    raw_weight(0, raw_qkv, qkv_w.rearrange("(k p) n -> p k n", p=P))
                    sp.dma_start(qk_bias[:, :], qkv_b[0:2 * C].rearrange("(k p) -> p k", p=P),
                                 allow_slow_non_contiguous=True).then_inc(bias_in, 16)
                    sp.dma_start(v_bias[:, :], qkv_b[2 * C:3 * C].partition_broadcast(P)).then_inc(bias_in, 16)
                    sp.dma_start(p_bias[:, :], proj_b.partition_broadcast(P)).then_inc(bias_in, 16)
                    raw_weight(1, raw_p, proj_w.rearrange("(k p) n -> p k n", p=P))
                    raw_weight(2, raw_g.bitcast(I32).rearrange("p (k n) -> p k n", n=C),
                               w_gate.rearrange("(k p) n -> p k n", p=P))
                    raw_weight(3, raw_u.bitcast(I32).rearrange("p (k n) -> p k n", n=C),
                               w_up.rearrange("(k p) n -> p k n", p=P))
                    sp.wait_ge(w_high, 2)
                    sp.wait_ge(w_low, 2)
                    raw_weight(4, raw_d.bitcast(I32).rearrange("p (k n) -> p k n", n=HID),
                               w_down.rearrange("(k p) n -> p k n", p=P))
                if row.has(0):
                    if row.has(1):
                        sp.wait_ge(dense_done, count(of_row(row, -1), ALL, kind="xn", index=1))
                        load_x(row.at + 1)
                    load_max(row, 1)
                if row.like == ROWS:
                    for half in range(2):
                        tiles = slice(half * NT // 2, (half + 1) * NT // 2)
                        sp.wait_ge(dense_free, count(row, ALL, kind="proj", index=half))
                        sp.dma_start(out_rows[row.at - 1, :, tiles], resid[:, tiles, :]).then_inc(out_done, 16)
                    sp.wait_ge(out_done, 16 * (row.at + 1))
                elif row.has(-1):
                    sp.wait_ge(dense_free, count(row, ALL, kind="proj", index=1))
                    sp.dma_start(out_rows[row.at - 1], resid[:, :, :]).then_inc(out_done, 16)
                    sp.wait_ge(out_done, 16 * row.at)
                if row.has(0):
                    sp.dma_start(resid[:, :, :], x_rows[row.at]).then_inc(resid_in, 16)
                    load_max(row, 2)
                if row.has(1):
                    spread_heads(row, 0)
                    heads_spread(row, 0)
                    load_stack(row, 0)
                    load_stack(row, 1)
                    spread_heads(row, 1)
                if row.has(0):
                    load_max(row, 3, meanwhile=1 if row.has(1) else None)
                elif row.has(1):
                    heads_spread(row, 1)
                if row.has(1):
                    load_stack(row, 2)
                    load_max(row, 0)
                    load_stack(row, 3)

            rows_of(sp, step)

        @block.gpsimd
        def _(pool):
            nc.gpsimd.memset(ident[:, :], 0.0).then_inc(ident_zero, 1)
            pool.wait_ge(ident_zero, 1)
            nc.gpsimd.affine_select(out=ident[:, :], in_=ident[:, :], compare_op=ALU.not_equal, fill=1.0, base=0,
                                    pattern=[[-1, P]], channel_multiplier=1).then_inc(ident_ready, 1)
            nc.gpsimd.memset(minus_half[:, :], -0.5)
            nc.gpsimd.memset(eps[:, :], EPS).then_inc(const_pool, 1)
            pool.wait_ge(const_pool, 1)

            def deviation(row):
                n = row.at + 1
                pool.wait_ge(moments_done, NT * (n + 1))
                nc.gpsimd.tensor_tensor(rstd[:, :], moments[:, :, 1], eps[:, :], ALU.add).then_inc(var_done, 1)
                pool.wait_ge(var_done, n + 1)
                nc.gpsimd.tensor_tensor(rstd[:, :], rstd[:, :], minus_half[:, :], ALU.pow).then_inc(rstd_done, 1)

            def hidden_low(row, chunk):
                n = count(row, ("up",), chunk)
                pool.wait_ge(dense_free, count(row, ALL, chunk))
                pool.wait_ge(hid_high, n)
                m = chunk[3]
                nc.gpsimd.tensor_tensor(hid_t[1][:, m, :], hid[:, m % 2, :], hid_t[0][:, m, :].bitcast(F32),
                                        ALU.subtract).then_inc(hid_low, 1)

            def step(row):
                if row.like == -1:
                    deviation(row)
                    pool.wait_ge(rstd_done, 1)
                    for g in range(NG):
                        nc.gpsimd.memset(k_stack[64:P, g].bitcast(F32), 1.0).then_inc(const_pool, 1)
                        pool.wait_ge(const_pool, 2 * g + 2)
                        nc.gpsimd.memset(q_stack[64:ONES_ROW, g].bitcast(F32), 0.0).then_inc(const_pool, 1)
                        pool.wait_ge(const_pool, 2 * g + 3)
                for s in range(STEPS):
                    if s == AVERAGE_AT // 4 and row.has(1) and row.like >= 0:
                        deviation(row)
                    if s == 9 and row.like == -1:
                        pool.wait_ge(dense_done, count(row, ALL, kind="wup", index=2))
                        nc.gpsimd.memset(v_ones[:, :, :, :], 1.0).then_inc(const_pool, 1)
                    if s == 5 and row.has(0):
                        pool.wait_ge(resid_in, 16 * (row.at + 1))
                        pool.wait_ge(bias_in, 48)
                        for t in range(NT):
                            nc.gpsimd.tensor_tensor(resid[:, t, :], resid[:, t, :], p_bias[:, :],
                                                    ALU.add).then_inc(resid_ready, 1)
                    for slot in range(4):
                        for chunk in chunks_at(row, s, slot):
                            if chunk[2] == "up":
                                hidden_low(row, chunk)

            rows_of(pool, step)

        @block.scalar
        def _(act):
            def split_high(n, dst, src):
                act.wait_ge(w_in[n], 16)
                nc.scalar.activation(dst, src, ACT.Copy).then_inc(w_high, 1)

            def exp(row, s, j):
                tile = 64 * row.at + 4 * s + j
                act.wait_ge(st_done, tile + 1)
                if j == 0 and 16 * row.like + s >= 2:
                    act.wait_ge(pv_done, 16 * row.at + s - 1)
                if row.like == 0 and s < 2:
                    act.wait_ge(squares_done, 3)
                nc.scalar.activation(probs[:, s % 2, j, :], transposed_bank(row, s, j)[:, :], ACT.Exp,
                                     scale=SCALE).then_inc(exp_done, 1)

            def take(row, chunk):
                _, _, kind, i, _ = chunk
                bank = bank_of(row, chunk)
                act.wait_ge(dense_done, count(row, ALL, chunk))
                if kind == "xn":
                    nc.scalar.activation(xn_t[0][:, i, :], bank[:, :], ACT.Copy).then_inc(act_done, 1)
                elif kind in ("q", "k"):
                    which = 0 if kind == "q" else 1
                    if row.has(0) or i == 1:
                        act.wait_ge(spread[1 - i], 80 * (row.at + 1 + i))
                    act.wait_ge(bias_in, 48)
                    nc.scalar.activation(qk_parts[:, which, 0, :], bank[:, :], ACT.Identity,
                                         bias=qk_bias[:, KC * which + i:KC * which + i + 1]).then_inc(act_done, 1)
                elif kind == "max":
                    g = 4 * (row.at + chunk[4]) + i
                    if 4 * (row.like + chunk[4]) + i >= 1:
                        act.wait_ge(max_in[(i - 1) % NG], 32 * (row.at + (1 if i else 0) + chunk[4]))
                    nc.scalar.activation(max_t[0][:, :], bank[0:HG * NT, 0:P], ACT.Copy).then_inc(act_done, 1)
                elif kind == "ot":
                    if i == 0:
                        act.wait_ge(spread[1], 80 * (row.at + (1 if row.has(0) else 0)))
                    nc.scalar.activation(qk_parts[:, i, 0, :], bank[:, :], ACT.Copy).then_inc(act_done, 1)
                elif kind == "gate":
                    if count(Row(row.like, row.like), ("gate",), chunk) > 1:
                        ups = [c for c in CHUNKS[:CHUNKS.index(chunk)] if c[2] == "up"]
                        if ups:
                            act.wait_ge(dense_free, count(row, ALL, ups[-1]))
                        else:
                            last_up = [c for c in CHUNKS if c[2] == "up"][-1]
                            act.wait_ge(dense_free, count(of_row(row, -1), ALL, last_up))
                    nc.scalar.activation(gated[:, :], bank[:, :], ACT.Tanh, scale=0.5 * QUANT).then_inc(act_done, 1)
                else:
                    w, cols = weight_place(kind, i)
                    nc.scalar.activation(w[0][cols], bank[:, :].rearrange("p (a n) -> p a n", a=2),
                                         ACT.Copy).then_inc(act_done, 1)

            def square_lows():
                act.wait_ge(dense_free, count(Row(-1, -1), ALL, kind="wdown", index=2))
                for n, w in enumerate((w_g, w_u, w_d)):
                    if n:
                        act.wait_ge(squares_done, n)
                    low = w[1][:, :, :].rearrange("p k n -> p (k n)").bitcast(F32)
                    nc.scalar.activation(raw[:, 0:KH * C], low, ACT.Square,
                                         accum_out=low_squares[:, n:n + 1]).then_inc(squares_done, 1)

            def hidden_high(row, chunk):
                act.wait_ge(dense_free, count(row, ALL, chunk))
                m = chunk[3]
                nc.scalar.activation(hid_t[0][:, m, :], hid[:, m % 2, :], ACT.Copy).then_inc(hid_high, 1)

            def step(row):
                if row.like == -1:
                    split_high(0, w_qkv[0][:, :, 0:C], raw_qkv[:, :, 0:C])
                    split_high(0, w_qkv[0][:, :, C:3 * C], raw_qkv[:, :, C:3 * C])
                    split_high(1, w_p[0][:, :, :], raw_p)
                for s in range(STEPS):
                    for slot in range(4):
                        if row.has(0):
                            exp(row, s, slot)
                        for r in (of_row(row, -1), row):
                            before = STEPS * 4 * (row.like - r.like) + 4 * s + slot - HIGH_DELAY
                            for chunk in CHUNKS:
                                if chunk[2] == "up" and r.like >= 0 and r.exists(chunk):
                                    if 4 * chunk[0] + chunk[1] == before:
                                        hidden_high(r, chunk)
                        for chunk in chunks_at(row, s, slot):
                            if chunk[2] in ON_ACT:
                                take(row, chunk)
                            if row.like == -1 and chunk[2] == "up":
                                hidden_high(row, chunk)
                            if row.like == -1 and chunk[2:4] == SQUARES_AFTER:
                                square_lows()
                        if slot == O_SLOT and s % NT == 0 and 0 < 16 * row.like + s <= 16 * ROWS:
                            act.wait_ge(pv_done, 16 * row.at + s)
                            if 16 * row.like + s > 4:
                                g = (s // NT - 2) % NG
                                shift = -1 if s == 0 else 0
                                act.wait_ge(dense_done, count(of_row(row, shift), ALL, kind="o", index=g))
                            nc.scalar.activation(o_raw[:, :], o_bank[:, :], ACT.Copy).then_inc(o_raw_done, 1)

            rows_of(act, step)

        @block.vector
        def _(dve):
            def statistics(row, t):
                if row.like == -1 and t % 2 == 0:
                    dve.wait_ge(x0_in[t // 2], 16)
                elif t == 0:
                    dve.wait_ge(x_in, 16 * (row.at + 1))
                nc.vector.bn_stats(stats[:, t, :], xn[:, t, :]).then_inc(stats_done, 1)

            def statistics_done(row):
                dve.wait_ge(stats_done, NT * (row.at + 2))

            def average():
                for t in range(NT):
                    nc.vector.bn_aggr(moments[:, t, :], stats[:, t, :]).then_inc(moments_done, 1)

            def normalise(row, t):
                if t == 0:
                    dve.wait_ge(rstd_done, row.at + 2)
                nc.vector.tensor_scalar(xn[:, t, :], xn[:, t, :], moments[:, t, 0:1], rstd[:, t:t + 1],
                                        ALU.subtract, ALU.mult).then_inc(xn_done, 1)

            def maximum(row, s, q):
                g, h, item, ahead = head_ahead(row, s)
                dve.wait_ge(s_done, 4 * item + q + 1)
                nc.vector.tensor_reduce(neg_max[:, g % 2, NT * h + q:NT * h + q + 1], score_bank(row, q)[:, :], AX_X,
                                        ALU.max, negate=True).then_inc(max_done, 1)

            def take(row, chunk):
                _, _, kind, i, offset = chunk
                bank = bank_of(row, chunk)
                if kind in ON_ACT:
                    dve.wait_ge(act_done, count(row, ON_ACT, chunk))
                else:
                    dve.wait_ge(dense_done, count(row, ALL, chunk))
                if kind == "xn":
                    nc.vector.tensor_tensor(xn_t[1][:, i, :], bank[:, :], xn_t[0][:, i, :].bitcast(F32),
                                            ALU.subtract).then_inc(dense_free, 1)
                elif kind in ("q", "k"):
                    which = 0 if kind == "q" else 1
                    nc.vector.scalar_tensor_tensor(qk_parts[:, which, 1, :], bank[:, :],
                                                   qk_bias[:, KC * which + i:KC * which + i + 1],
                                                   qk_parts[:, which, 0, :].bitcast(F32),
                                                   ALU.add, ALU.subtract).then_inc(dense_free, 1)
                elif kind == "v":
                    if i == 0 and row.has(-1):
                        dve.wait_ge(pv_done, 16 * row.at)
                    if i == 0 and row.like == 0:
                        dve.wait_ge(const_pool, 2 * NG + 2)
                        dve.wait_ge(bias_in, 48)
                    for u in range(2):
                        done = nc.vector.tensor_tensor(v_ones[:, 2 * i + u, :, 0:HD],
                                                       bank[:, C * u:C * (u + 1)].rearrange("p (h d) -> p h d", d=HD),
                                                       v_bias[:, :].rearrange("p (h d) -> p h d", d=HD), ALU.add)
                    done.then_inc(dense_free, 1)
                elif kind == "max":
                    nc.vector.tensor_tensor(max_t[1][:, :], bank[0:HG * NT, 0:P], max_t[0][:, :].bitcast(F32),
                                            ALU.subtract).then_inc(dense_free, 1)
                elif kind == "o":
                    heads = bank[:, :].rearrange("p (t h d) -> p t h d", t=NT, h=HG)
                    if 4 * (row.like + offset) + i >= 1:
                        dve.wait_ge(dense_free, count(row, ALL, chunk) - 1)
                    nc.vector.reciprocal(inv_sum[:, :, :], heads[:, :, :, HD]).then_inc(inv_done, 1)
                    dve.wait_ge(inv_done, 4 * (row.at + offset) + i + 1)
                    nc.vector.tensor_tensor(
                        o_norm[:, :, HG * HD * i:HG * HD * (i + 1)].rearrange("p t (h d) -> p t h d", d=HD),
                        heads[:, :, :, 0:HD], inv_sum[:, :, :].unsqueeze(3).broadcast_to([P, NT, HG, HD]),
                        ALU.mult).then_inc(dense_free, 1)
                elif kind == "ot":
                    nc.vector.tensor_tensor(qk_parts[:, i, 1, :], bank[:, :], qk_parts[:, i, 0, :].bitcast(F32),
                                            ALU.subtract).then_inc(dense_free, 1)
                elif kind == "gate":
                    nc.vector.scalar_tensor_tensor(gated[:, :], gated[:, :], 1.0, bank[:, :], ALU.add,
                                                   ALU.mult).then_inc(dense_free, 1)
                elif kind == "up":
                    n = count(row, ("up",), chunk)
                    if count(Row(row.like, row.like), ("up",), chunk) > 2:
                        dve.wait_ge(hid_high, n - 2)
                        dve.wait_ge(hid_low, n - 2)
                    dve.wait_ge(dense_free, count(row, ALL, kind="gate", index=i))
                    nc.vector.scalar_tensor_tensor(hid[:, i % 2, :], bank[:, :], 0.5 * QUANT ** 3, gated[:, :],
                                                   ALU.mult, ALU.mult).then_inc(dense_free, 1)
                elif kind == "down":
                    if i == 0:
                        dve.wait_ge(resid_ready, NT * (row.at + 1))
                    nc.vector.tensor_tensor(resid[:, i, :], bank[:, 0:C], resid[:, i, :],
                                            ALU.add).then_inc(dense_free, 1)
                elif kind == "proj":
                    if i == 0:
                        dve.wait_ge(dense_free, count(of_row(row, -1), ALL, kind="down", index=3))
                    both = resid[:, 2 * i:2 * i + 2, :]
                    nc.vector.tensor_tensor(both, bank[:, :].rearrange("p (t n) -> p t n", t=2), both,
                                            ALU.add).then_inc(dense_free, 1)
                else:
                    w, cols = weight_place(kind, i)
                    nc.vector.tensor_tensor(w[1][cols],
                                            bank[:, :].rearrange("p (a n) -> p a n", a=2),
                                            w[0][cols].bitcast(F32), ALU.subtract).then_inc(dense_free, 1)

            def split_low(n, dst, src, high):
                dve.wait_ge(w_high, n)
                nc.vector.tensor_tensor(dst, src, high.bitcast(F32), ALU.subtract).then_inc(w_low, 1)

            def to_float(n, ints):
                dve.wait_ge(w_in[n], 16)
                nc.vector.tensor_copy(ints, ints.bitcast(I32)).then_inc(w_float, 1)

            def prepare(after):
                if after == ("xn", 1):
                    kv = slice(C, 3 * C)
                    split_low(2, w_qkv[1][:, :, kv], raw_qkv[:, :, kv], w_qkv[0][:, :, kv])
                    to_float(2, raw_g)
                elif after == ("q", 0):
                    to_float(3, raw_u)
                elif after == ("wgate", 2):
                    to_float(4, raw_d)
                elif after == ("wdown", 2):
                    split_low(3, w_p[1][:, :, :], raw_p, w_p[0][:, :, :])
                elif after == DECISION_AFTER:
                    decide()

            def decide():
                dve.wait_ge(squares_sum, 1)
                nc.vector.tensor_scalar(all_exact[:, :], o_bank[0:1, 0:1], 0.0, None,
                                        ALU.is_equal).then_inc(exact_known, 1)

            def step(row):
                if row.like == -1:
                    for t in range(NT):
                        statistics(row, t)
                    statistics_done(row)
                    average()
                    for t in range(NT):
                        normalise(row, t)
                    split_low(1, w_qkv[1][:, :, 0:C], raw_qkv[:, :, 0:C], w_qkv[0][:, :, 0:C])
                for s in range(STEPS):
                    for slot in range(4):
                        at = 4 * s + slot
                        layernorm = row.like >= 0 and row.has(1)
                        if layernorm and 0 <= at - STATS_AT < NT:
                            statistics(row, at - STATS_AT)
                        if layernorm and 0 <= at - NORMALISE_AT < NT:
                            normalise(row, at - NORMALISE_AT)
                        if layernorm and at == AVERAGE_AT:
                            statistics_done(row)
                        if head_ahead(row, s):
                            maximum(row, s, slot)
                        if layernorm and at == AVERAGE_AT:
                            average()
                        for chunk in chunks_at(row, s, slot):
                            take(row, chunk)
                            if row.like == -1:
                                prepare(chunk[2:4])

            rows_of(dve, step)

        @block.tensor
        def _(pe):
            SPLIT = ((0, 0), (1, 0), (0, 1))
            STATIONARY_EXACT = ((0, 0), (0, 1))
            MOVING_EXACT = ((0, 0), (1, 0))

            def scores_t(row, s, j):
                g, kt = s // NT, s % NT
                tile = 64 * row.at + 4 * s + j
                if kt == 0 and j == 0:
                    pe.wait_ge(max_in[g], 32 * (row.at + 1))
                if after_scores(row, s - 1):
                    pe.wait_ge(exp_done, tile - 3)
                elif after_scores(row, s) and j >= 2:
                    pe.wait_ge(max_done, NT * HEADS * ROWS - 3 + j)
                elif 16 * row.like + s > 0 or j >= 2:
                    pe.wait_ge(exp_done, tile - 1)
                else:
                    pe.wait_ge(max_done, 4 * LEAD - 1 + j)
                nc.tensor.matmul(transposed_bank(row, s, j)[:, :], k_stack[0:STACK, g, j, P * kt:P * (kt + 1)],
                                 q_stack[0:STACK, g, j, :], start=True, stop=True).then_inc(st_done, 1)

            def scores(row, s, q):
                g, h, item, ahead = head_ahead(row, s)
                if h == 0 and q == 0:
                    pe.wait_ge(stack_in[g], 64 * (row.at + ahead + 1))
                    if row.like + ahead == 0:
                        pe.wait_ge(const_pool, 2 * g + 3)
                if row.like >= 0:
                    pe.wait_ge(max_done, 4 * item + q - 1)
                elif STEPS * row.like + s + LEAD > 0:
                    pe.wait_ge(max_done, 4 * item + q - 3)
                nc.tensor.matmul(score_bank(row, q)[:, :], q_stack[0:ONES_ROW, g, h, P * q:P * (q + 1)],
                                 k_stack[0:ONES_ROW, g, h, :], start=True, stop=True).then_inc(s_done, 1)

            def probs_v(row, s):
                g, kt = (s - 1) % STEPS // NT, (s - 1) % NT
                n = 16 * row.at + s
                pe.wait_ge(exp_done, 4 * n)
                if s == 1:
                    pe.wait_ge(dense_free, count(row, ALL, kind="v", index=1))
                if kt == 0 and 16 * row.like + s > 1:
                    pe.wait_ge(o_raw_done, 4 * row.at + s // NT)
                for j in range(HG):
                    done = nc.tensor.matmul(o_bank[32 * j:32 * (j + 1), :], v_ones[:, kt, HG * g + j, :],
                                            probs[:, (s - 1) % 2, j, :], start=kt == 0, stop=kt == NT - 1,
                                            tile_position=(0, 32 * j))
                done.then_inc(pv_done, 1)

            def product(bank, stationary, moving, tiles, parts=SPLIT):
                for n, (a, b) in enumerate(parts):
                    for k in range(tiles):
                        done = nc.tensor.matmul(bank, stationary(a, k), moving(b, k), start=n == 0 and k == 0,
                                                stop=n == len(parts) - 1 and k == tiles - 1)
                return done

            def chunk_products(row, chunk, exact):
                _, _, kind, i, offset = chunk
                bank = bank_of(row, chunk)
                n = count(row, ALL, chunk)
                if count(Row(row.like, row.like), ALL, chunk) > DENSE_BANKS:
                    pe.wait_ge(dense_free, n - DENSE_BANKS)
                if kind == "xn":
                    if i == 0:
                        pe.wait_ge(xn_done, NT * (row.at + 2))
                    for t in range(NT):
                        done = nc.tensor.transpose(bank[:, P * t:P * (t + 1)], xn[:, t, P * i:P * (i + 1)], ident[:, :])
                elif kind in ("q", "k"):
                    if kind == "q" and i == 0:
                        pe.wait_ge(dense_free, count(row, ALL, kind="xn", index=1))
                    if i == 0 and row.like == -1:
                        pe.wait_ge(w_low, 1 if kind == "q" else 2)
                    base = (0 if kind == "q" else C) + P * i
                    done = product(bank[:, :], lambda a, k: w_qkv[a][:, k, base:base + P],
                                   lambda b, k: xn_t[b][:, k, :], KC)
                elif kind == "v":
                    for u in range(2):
                        t = 2 * i + u
                        done = product(bank[:, C * u:C * (u + 1)], lambda a, k: xn_t[a][:, k, P * t:P * (t + 1)],
                                       lambda b, k: w_qkv[b][:, k, 2 * C:3 * C], KC)
                elif kind == "max":
                    pe.wait_ge(max_done, 16 * (4 * (row.at + offset) + i + 1))
                    done = nc.tensor.transpose(bank[0:HG * NT, 0:P], neg_max[:, i % 2, :], ident[:, :])
                elif kind == "o":
                    pe.wait_ge(o_raw_done, 4 * (row.at + offset) + i + 1)
                    for t in range(NT):
                        done = nc.tensor.transpose(bank[:, P * t:P * (t + 1)], o_raw[:, P * t:P * (t + 1)], ident[:, :])
                elif kind == "ot":
                    if i == 0:
                        pe.wait_ge(dense_free, count(row, ALL, kind="o", index=3))
                    for t in range(NT):
                        done = nc.tensor.transpose(bank[:, P * t:P * (t + 1)], o_norm[:, t, P * i:P * (i + 1)],
                                                   ident[:, :])
                elif kind in ("gate", "up"):
                    w = w_g if kind == "gate" else w_u
                    if kind == "gate" and count(Row(row.like, row.like), ("gate",), chunk) == 1:
                        pe.wait_ge(dense_free, count(Row(-1, -1), ALL, kind="wdown", index=2))
                    done = product(bank[:, :], lambda a, k: w[a][:, k, P * i:P * (i + 1)],
                                   lambda b, k: xn_t[b][:, k, :], KC, STATIONARY_EXACT if exact else SPLIT)
                elif kind == "down":
                    if i == 0:
                        pe.wait_ge(hid_high, KH * (row.at + 1))
                        pe.wait_ge(hid_low, KH * (row.at + 1))
                    done = product(bank[:, 0:C], lambda a, k: hid_t[a][:, k, P * i:P * (i + 1)],
                                   lambda b, k: w_d[b][:, k, :], KH, MOVING_EXACT if exact else SPLIT)
                elif kind == "proj":
                    for u in range(2):
                        t = 2 * i + u
                        for k in range(KC):
                            if i == 0 and u == 0:
                                pe.wait_ge(dense_free, count(row, ALL, kind="ot", index=k))
                            for n, (a, b) in enumerate(SPLIT):
                                done = nc.tensor.matmul(bank[:, C * u:C * (u + 1)],
                                                        qk_parts[:, k, a, P * t:P * (t + 1)], w_p[b][:, k, :],
                                                        start=k == 0 and n == 0,
                                                        stop=k == KC - 1 and n == len(SPLIT) - 1)
                elif kind == "wdown":
                    pe.wait_ge(w_float, 3)
                    d = raw_d.rearrange("p (k n) -> p k n", n=HID)
                    for t in range(4):
                        m, c = 2 * i + t // 2, t % 2
                        done = nc.tensor.transpose(bank[:, P * t:P * (t + 1)], d[:, c, P * m:P * (m + 1)], ident[:, :])
                else:
                    pe.wait_ge(w_float, 1 if kind == "wgate" else 2)
                    w = (raw_g if kind == "wgate" else raw_u).rearrange("p (k n) -> p k n", n=C)
                    for t in range(4):
                        c, m = t // 2, 2 * i + t % 2
                        done = nc.tensor.transpose(bank[:, P * t:P * (t + 1)], w[:, m, P * c:P * (c + 1)], ident[:, :])
                done.then_inc(dense_done, 1)

            def sum_squares():
                pe.wait_ge(squares_done, 3)
                for n in range(3):
                    done = nc.tensor.matmul(o_bank[0:1, 0:1], minus_half[:, 0:1], low_squares[:, n:n + 1],
                                            start=n == 0, stop=n == 2)
                done.then_inc(squares_sum, 1)

            def stay_busy(turns):
                for _ in range(turns):
                    nc.tensor.transpose(st_bank[0][:, 0:P], ident[:, :], ident[:, :])

            def step(row, exact):
                for s in range(STEPS):
                    for slot in range(4):
                        if row.has(0):
                            scores_t(row, s, slot)
                        if slot == PV_SLOT and 0 < 16 * row.like + s <= 16 * ROWS:
                            probs_v(row, s)
                            if row.like == ROWS:
                                stay_busy(BUSY_AFTER["last"])
                        if row.like == -1 and head_ahead(row, s):
                            scores(row, s, slot)
                        for chunk in chunks_at(row, s, slot):
                            chunk_products(row, chunk, exact)
                            if row.like == ROWS:
                                stay_busy(BUSY_AFTER.get(chunk[2:4], 0))
                            if row.like == -1 and chunk[2:4] == DECISION_AFTER:
                                sum_squares()
                        if row.like >= 0 and head_ahead(row, s):
                            scores(row, s, slot)

            def rows_from_0(exact):
                step(Row(0, 0), exact)
                with pe.Fori(1, ROWS - 1) as b:
                    step(Row(b, 1), exact)
                step(Row(ROWS - 1, ROWS - 1), exact)
                step(Row(ROWS, ROWS), exact)

            pe.wait_ge(ident_ready, 1)
            with pe.Fori(0, WARM_UP):
                for t in range(NT):
                    nc.tensor.transpose(o_bank[:, P * t:P * (t + 1)], ident[:, :], ident[:, :])
            step(Row(-1, -1), False)
            pe.wait_ge(exact_known, 1)
            flag = pe.value_load(all_exact[0:1, 0:1], min_val=0, max_val=1)
            with pe.If(flag == 1):
                rows_from_0(True)
            with pe.Else():
                rows_from_0(False)


_INS = ["L0_attn_x", "L0_attn_qkv_w", "L0_attn_qkv_b", "L0_attn_proj_w", "L0_attn_proj_b",
        "L0_ffn_w_gate", "L0_ffn_w_up", "L0_ffn_w_down"]


def kernel(**inputs):
    import numpy as _np
    import concourse.bacc as _bacc
    from concourse import mybir as _mybir
    from concourse.bass_utils import run_bass_kernel_spmd as _run

    nc = _bacc.Bacc("TRN2", target_bir_lowering=False, num_devices=1)
    arrays, args = {}, []
    for name in _INS:
        a = _np.ascontiguousarray(inputs[name])
        arrays[f"in_{name}"] = a
        args.append(nc.dram_tensor(f"in_{name}", a.shape, _mybir.dt.from_np(a.dtype), kind="ExternalInput").ap())
    out = nc.dram_tensor("out_0", (ROWS, TOK, C), F32, kind="ExternalOutput").ap()
    build(nc, *args, out)
    r = _run(nc, [arrays], core_ids=[0])
    return r.results[0]["out_0"]
```
